# Optimizing a Trainium2 kernel written in Bass

```python
import numpy as np
import jax
import jax.numpy as jnp

def _softmax(x, axis=-1):
    return jax.nn.softmax(x, axis=axis)

def _gelu(x):
    return jax.nn.gelu(x, approximate=True)

def _silu(x):
    return jax.nn.silu(x)

def _sigmoid(x):
    return jax.nn.sigmoid(x)

def _layernorm(x, axis=-1, eps=1e-05):
    m = jnp.mean(x, axis=axis, keepdims=True)
    v = jnp.var(x, axis=axis, keepdims=True)
    return (x - m) / jnp.sqrt(v + eps)

def _scatter_add(tgt, idx, src, axis=0):
    return tgt.at[idx].add(src)

def _segment_sum(src, seg, n):
    return jax.ops.segment_sum(src, seg, n)
kernel_name = 'mk_decoder_postln_d1_seqx_r2_c65682'

def setup_inputs(seed: int=0):
    np.random.seed(seed)
    _w = jnp.asarray

    def _rec_inputs():
        import jax
        import jax.numpy as jnp
        _rk = jax.random.key(seed)
        x = -0.0002928 + 1 * jax.random.normal(jax.random.fold_in(_rk, 1), (2, 2048, 512), jnp.float32)
        _lenS = 2048 - jax.random.randint(jax.random.fold_in(_rk, 7), (2,), 0, max(1, 2048 // 4) + 1, jnp.int32)
        _lenS2 = 154 - jax.random.randint(jax.random.fold_in(_rk, 8), (2,), 0, max(1, 154 // 4) + 1, jnp.int32)
        _ctx_1024P = jax.random.normal(jax.random.fold_in(_rk, 11), (2, 16, 512), jnp.float32)
        _ctx_1024c = jax.random.dirichlet(jax.random.fold_in(_rk, 511), 0.3 * jnp.ones((16,), jnp.float32), (2, 154))
        _ctx_1024t = jnp.einsum('bsk,bkd->bsd', _ctx_1024c, _ctx_1024P)
        _ctx_1024t = _ctx_1024t * jax.lax.rsqrt(jnp.mean(jnp.square(_ctx_1024t)) + 1e-12) * 0.953939
        ctx_1024 = -1.39393e-06 + 0.999914 * (_ctx_1024t + 0.3 * jax.random.normal(jax.random.fold_in(_rk, 611), (2, 154, 512), jnp.float32))
        _validS = jnp.arange(2048)[None, :] < _lenS[:, None]
        _validS2 = jnp.arange(154)[None, :] < _lenS2[:, None]
        _causal = jnp.tril(jnp.ones((2048, 2048), dtype=bool))
        mask_Bx1xSxS2_ik1 = jnp.where(jnp.broadcast_to(_validS2[:, None, None, :], (2, 1, 2048, 154)), 1, 0).astype(jnp.int32)
        return (x, ctx_1024, mask_Bx1xSxS2_ik1)
    x, ctx_1024, mask_Bx1xSxS2_ik1 = _rec_inputs()

    def _L0_attn_setup():
        import jax, jax.numpy as jnp
        import numpy as np
        B, N, D, H = (2, 1024, 512, 8)
        DH = D // H
        key = jax.random.key(seed)
        k0, k1, k2 = jax.random.split(key, 3)
        s = 1.0 / np.sqrt(D).astype(np.float32)
        return {'x': jax.random.normal(k0, (B, N, D), dtype=jnp.float32), 'w_qkv': jax.random.normal(k1, (3 * D, D), dtype=jnp.float32) * s, 'b_qkv': jnp.zeros((3 * D,), dtype=jnp.float32), 'w_o': jax.random.normal(k2, (D, D), dtype=jnp.float32) * s, 'b_o': jnp.zeros((D,), dtype=jnp.float32)}
    _L0_attn_all = _L0_attn_setup()
    _L0_attn_in = {k: v for k, v in _L0_attn_all.items() if k in ('w_qkv', 'b_qkv', 'w_o', 'b_o')}
    del _L0_attn_all

    def _L0_xattn_setup():
        import jax, jax.numpy as jnp
        import numpy as np
        D_MODEL = 512
        NUM_HEADS = 16
        D_K = D_MODEL // NUM_HEADS
        NEG_INF = -1000000000.0

        def _split_heads(x):
            B, S, _ = x.shape
            return x.reshape(B, S, NUM_HEADS, D_K).transpose(0, 2, 1, 3)
        key = jax.random.key(seed)
        ks = jax.random.split(key, 13)
        B, S = (2, 1024)
        scale = 1.0 / np.sqrt(D_MODEL)
        inp = {'Query': jax.random.normal(ks[0], (B, S, D_MODEL), jnp.float32), 'Key': jax.random.normal(ks[1], (B, S, D_MODEL), jnp.float32), 'Values': jax.random.normal(ks[2], (B, S, D_MODEL), jnp.float32), 'Mask': jax.random.randint(ks[3], (B, 1, S, S), 0, 2, jnp.int32), 'W_q': jax.random.normal(ks[4], (D_MODEL, D_MODEL), jnp.float32) * scale, 'b_q': jnp.zeros((D_MODEL,), jnp.float32), 'W_k': jax.random.normal(ks[5], (D_MODEL, D_MODEL), jnp.float32) * scale, 'b_k': jnp.zeros((D_MODEL,), jnp.float32), 'W_v': jax.random.normal(ks[6], (D_MODEL, D_MODEL), jnp.float32) * scale, 'b_v': jnp.zeros((D_MODEL,), jnp.float32), 'W_o': jax.random.normal(ks[7], (D_MODEL, D_MODEL), jnp.float32) * scale, 'b_o': jnp.zeros((D_MODEL,), jnp.float32)}
        return inp
    _L0_xattn_all = _L0_xattn_setup()
    _L0_xattn_in = {k: v for k, v in _L0_xattn_all.items() if k in ('W_q', 'b_q', 'W_k', 'b_k', 'W_v', 'b_v', 'W_o', 'b_o')}
    del _L0_xattn_all

    def _L0_ffn_setup():
        import jax, jax.numpy as jnp
        import numpy as np
        DIM = 512

        def _reference_tuple_inner(x, W_r, W_k, W_v, mu_r, mu_k):
            B, T, C = x.shape
            x_prev = jnp.concatenate([jnp.zeros((B, 1, C), x.dtype), x[:, :-1, :]], axis=1)
            xr = mu_r * x + (1.0 - mu_r) * x_prev
            xk = mu_k * x + (1.0 - mu_k) * x_prev
            r = jax.nn.sigmoid(jnp.einsum('btc,dc->btd', xr, W_r))
            k = jnp.einsum('btc,dc->btd', xk, W_k)
            k_act = jnp.square(jax.nn.relu(k))
            out = r * jnp.einsum('btc,dc->btd', k_act, W_v)
            new_state = x[:, -1, :]
            return (out, new_state)
        key = jax.random.key(seed)
        ks = jax.random.split(key, 6)
        B, T, C = (8, 1024, DIM)
        x = jax.random.normal(ks[0], (B, T, C), dtype=jnp.float32)
        s = 1.0 / np.sqrt(C)
        W_r = jax.random.uniform(ks[1], (C, C), jnp.float32, -s, s)
        W_k = jax.random.uniform(ks[2], (C, C), jnp.float32, -s, s)
        W_v = jax.random.uniform(ks[3], (C, C), jnp.float32, -s, s)
        mu_r = jax.random.uniform(ks[4], (C,), jnp.float32)
        mu_k = jax.random.uniform(ks[5], (C,), jnp.float32)
        return {'x': x, 'W_r': W_r, 'W_k': W_k, 'W_v': W_v, 'mu_r': mu_r, 'mu_k': mu_k}
    _L0_ffn_all = _L0_ffn_setup()
    _L0_ffn_in = {k: v for k, v in _L0_ffn_all.items() if k in ('W_r', 'W_k', 'W_v', 'mu_r', 'mu_k')}
    del _L0_ffn_all
    return {'x': x, 'ctx_1024': ctx_1024, 'mask_Bx1xSxS2_ik1': mask_Bx1xSxS2_ik1, 'L0_attn_w_qkv': _L0_attn_in['w_qkv'], 'L0_attn_b_qkv': _L0_attn_in['b_qkv'], 'L0_attn_w_o': _L0_attn_in['w_o'], 'L0_attn_b_o': _L0_attn_in['b_o'], 'L0_xattn_W_q': _L0_xattn_in['W_q'], 'L0_xattn_b_q': _L0_xattn_in['b_q'], 'L0_xattn_W_k': _L0_xattn_in['W_k'], 'L0_xattn_b_k': _L0_xattn_in['b_k'], 'L0_xattn_W_v': _L0_xattn_in['W_v'], 'L0_xattn_b_v': _L0_xattn_in['b_v'], 'L0_xattn_W_o': _L0_xattn_in['W_o'], 'L0_xattn_b_o': _L0_xattn_in['b_o'], 'L0_ffn_W_r': _L0_ffn_in['W_r'], 'L0_ffn_W_k': _L0_ffn_in['W_k'], 'L0_ffn_W_v': _L0_ffn_in['W_v'], 'L0_ffn_mu_r': _L0_ffn_in['mu_r'], 'L0_ffn_mu_k': _L0_ffn_in['mu_k']}

def reference(x, ctx_1024, mask_Bx1xSxS2_ik1, L0_attn_w_qkv, L0_attn_b_qkv, L0_attn_w_o, L0_attn_b_o, L0_xattn_W_q, L0_xattn_b_q, L0_xattn_W_k, L0_xattn_b_k, L0_xattn_W_v, L0_xattn_b_v, L0_xattn_W_o, L0_xattn_b_o, L0_ffn_W_r, L0_ffn_W_k, L0_ffn_W_v, L0_ffn_mu_r, L0_ffn_mu_k):
    import jax
    import jax.numpy as jnp

    def _L0_attn_ref(x, w_qkv, b_qkv, w_o, b_o):
        import jax, jax.numpy as jnp
        import numpy as np
        B, N, D, H = (2, 1024, 512, 8)
        DH = D // H
        b, n, d = x.shape
        h = H
        dh = d // h
        qkv = x @ w_qkv.T + b_qkv
        qkv = qkv.reshape(b, n, 3, dh, h)
        qkv = jnp.transpose(qkv, (2, 0, 4, 1, 3))
        q, k, v = (qkv[0], qkv[1], qkv[2])
        attn = jnp.einsum('bhik,bhjk->bhij', q, k)
        out = jnp.einsum('bhik,bhkj->bhij', attn, v)
        out = jnp.transpose(out, (0, 2, 1, 3)).reshape(b, n, d)
        return out @ w_o.T + b_o

    def _L0_xattn_ref(Query, Key, Values, Mask, W_q, b_q, W_k, b_k, W_v, b_v, W_o, b_o):
        import jax, jax.numpy as jnp
        import numpy as np
        D_MODEL = 512
        NUM_HEADS = 16
        D_K = D_MODEL // NUM_HEADS
        NEG_INF = -1000000000.0

        def _split_heads(x):
            B, S, _ = x.shape
            return x.reshape(B, S, NUM_HEADS, D_K).transpose(0, 2, 1, 3)
        q = _split_heads(Query @ W_q.T + b_q)
        k = _split_heads(Key @ W_k.T + b_k)
        v = _split_heads(Values @ W_v.T + b_v)
        scores = jnp.einsum('bhqd,bhkd->bhqk', q, k) / jnp.sqrt(jnp.float32(D_K))
        scores = jnp.where(Mask == 0, jnp.float32(NEG_INF), scores)
        attn = jax.nn.softmax(scores, axis=-1)
        out = jnp.einsum('bhqk,bhkd->bhqd', attn, v)
        B, H, S, Dk = out.shape
        out = out.transpose(0, 2, 1, 3).reshape(B, S, H * Dk)
        return out @ W_o.T + b_o

    def _L0_ffn_ref(x, W_r, W_k, W_v, mu_r, mu_k):
        import jax, jax.numpy as jnp
        import numpy as np
        DIM = 512

        def _reference_tuple_inner(x, W_r, W_k, W_v, mu_r, mu_k):
            B, T, C = x.shape
            x_prev = jnp.concatenate([jnp.zeros((B, 1, C), x.dtype), x[:, :-1, :]], axis=1)
            xr = mu_r * x + (1.0 - mu_r) * x_prev
            xk = mu_k * x + (1.0 - mu_k) * x_prev
            r = jax.nn.sigmoid(jnp.einsum('btc,dc->btd', xr, W_r))
            k = jnp.einsum('btc,dc->btd', xk, W_k)
            k_act = jnp.square(jax.nn.relu(k))
            out = r * jnp.einsum('btc,dc->btd', k_act, W_v)
            new_state = x[:, -1, :]
            return (out, new_state)
        return _reference_tuple_inner(x, W_r, W_k, W_v, mu_r, mu_k)[0]
    x = _layernorm(x + _L0_attn_ref(x, L0_attn_w_qkv, L0_attn_b_qkv, L0_attn_w_o, L0_attn_b_o), axis=-1)
    x = _layernorm(x + _L0_xattn_ref(x, ctx_1024, ctx_1024, mask_Bx1xSxS2_ik1, L0_xattn_W_q, L0_xattn_b_q, L0_xattn_W_k, L0_xattn_b_k, L0_xattn_W_v, L0_xattn_b_v, L0_xattn_W_o, L0_xattn_b_o), axis=-1)
    x = _layernorm(x + _L0_ffn_ref(x, L0_ffn_W_r, L0_ffn_W_k, L0_ffn_W_v, L0_ffn_mu_r, L0_ffn_mu_k), axis=-1)
    return x

_drawn_inputs = setup_inputs


def setup_inputs(seed=0):
    import zlib

    import numpy as np

    out = dict(_drawn_inputs(seed))
    spreads = {'L0_attn_b_qkv': (0.0, 0.1),
     'L0_attn_b_o': (0.0, 0.8),
     'L0_xattn_b_q': (0.0, 0.462),
     'L0_xattn_b_k': (0.0, 0.8),
     'L0_xattn_b_v': (0.0, 0.1),
     'L0_xattn_b_o': (0.0, 0.1)}
    factors = {'L0_ffn_W_r': 2.82, 'L0_ffn_mu_r': 6.838}
    for name, (base, spread) in spreads.items():
        noise = np.random.default_rng([zlib.crc32(name.encode()), seed]).standard_normal(out[name].shape)
        drawn = base * np.exp(spread * noise) if base else spread * noise
        out[name] = jnp.asarray(drawn.astype(out[name].dtype))
    for name, factor in factors.items():
        out[name] = (out[name] * factor).astype(out[name].dtype)
    return out
```

```python
import numpy as np
import concourse.bass as bass
from concourse import mybir
from concourse.alu_op_type import AluOpType as ALU

F32 = mybir.dt.float32
F32R = mybir.dt.float32r
I32 = mybir.dt.int32
ACT = mybir.ActivationFunctionType

P = 128
B, S, D = 2, 2048, 512
KT = D // P
CTX = 154
HEADS, DK = 16, D // 16
HPG = P // DK
HG = HEADS // HPG
GK = HPG * CTX
HALF = GK // 2
CH = -(-GK // P)
SELF_DH = 64
GT = 256
TPG = GT // P
NG = B * S // GT
UNITS = HG * TPG
EPS = 1e-5
SCALE = float(DK) ** -0.5
NEG = -float(2.0 ** 100)
HUGE = 3.0e38

COLS = ("self_bq", "self_bv", "cross_bq", "cross_bk", "mu_r", "mu_k")
ROWS = ("self_bk", "self_bv_row", "self_bo", "cross_bv", "cross_bo")


class Signal:

    def __init__(self, nc, ctx, name, per, producer, step=1):
        self.sem = ctx.enter_context(nc.semaphore(name))
        self.per, self.step = per, step
        producer.sem_inc(self.sem, per * step)

    def by(self, instruction):
        instruction.then_inc(self.sem, self.step)

    def wait(self, engine, n, k):
        engine.wait_ge(self.sem, (n * self.per + (self.per + k)) * self.step)


class Count:

    def __init__(self, nc, ctx, name, step=1):
        self.sem, self.n, self.step = ctx.enter_context(nc.semaphore(name)), 0, step

    def did(self, instruction):
        instruction.then_inc(self.sem, self.step)
        self.n += self.step
        return self.n

    def wait(self, engine, value=None):
        engine.wait_ge(self.sem, self.n if value is None else value)


class Map:

    def __init__(self, nc):
        self.nc, self.at, self.end = nc, -(-nc.sbuf_base // 32) * 32, nc.sbuf_usable_end

    def place(self, name, shape, dtype=F32):
        size = 4 * int(np.prod(shape[1:]))
        t = self.nc.alloc_sbuf_tensor_at(name, list(shape), dtype, offset=self.at)
        self.at += -(-size // 32) * 32
        assert self.at <= self.end, (name, self.at, self.end)
        return t

    def pair(self, name, shape):
        return self.place(name + "_hi", shape, F32R), self.place(name + "_lo", shape, F32R)

    def joined_pair(self, name, shape, axis):
        both = self.place(name, shape[:axis] + [2] + shape[axis:], F32R)
        half = lambda i: both[(slice(None),) * axis + (i,)]
        return both, half(0), half(1)


def f32(ap):
    return ap.bitcast(F32)


def three_pass(pe, out, sta, mov, first=True, last=True):
    pe.matmul(out, sta[0], mov[0], start=first, stop=False, skip_group_check=True)
    pe.matmul(out, sta[0], mov[1], start=False, stop=False, skip_group_check=True)
    return pe.matmul(out, sta[1], mov[0], start=False, stop=last, skip_group_check=True)


def context_and_gram(nc, io, mem, kv, col_sb, gram, fold_w):
    from contextlib import ExitStack

    x_sum, k_both, v_both = kv[4:]
    sp, act, pe, dve, pool = nc.sync, nc.scalar, nc.tensor, nc.vector, nc.gpsimd
    rows_of = [(r, min(P, B * CTX - r)) for r in range(0, B * CTX, P)]
    RING = 4
    with ExitStack() as ctx:
        ctx_t = mem.place("ctx_t", [P, KT, B * CTX])
        w_k = mem.place("w_k_raw", [P, KT, D])
        w_v = mem.place("w_v_raw", [P, KT, D])
        bv_row = mem.place("cross_bv_row", [P, D])
        kt, kt_hi, kt_lo = mem.joined_pair("kt", [P, KT, B * CTX], 1)
        v_raw = mem.place("v_raw", [P, len(rows_of), D])
        vn, vn_hi, vn_lo = mem.joined_pair("vn", [P, len(rows_of), D], 2)
        x_in = [mem.place(f"x_in{i}", [P, D]) for i in range(RING)]
        x_hi = [mem.place(f"x_hi{i}", [P, D], F32R) for i in range(RING)]
        x_lo = [mem.place(f"x_lo{i}", [P, D], F32R) for i in range(RING)]

        block = ctx.enter_context(nc.Block())
        loads = [Count(nc, ctx, f"ctx_load{i}", 16) for i in range(5)]
        weights_in = Count(nc, ctx, "fold_weights_in", 16)
        mm = Count(nc, ctx, "ctx_mm")
        on_dve = Count(nc, ctx, "ctx_dve")
        on_act = Count(nc, ctx, "ctx_act")
        zeroed = Count(nc, ctx, "kv_zeroed")
        placed = Count(nc, ctx, "kv_placed", 16)
        alone = ctx.enter_context(nc.semaphore("alone_gram"))

        def stands_alone(engine):
            engine.sem_inc(alone, 1)

        sum_zero = zeroed.did(pool.memset(x_sum[:], 0.0))
        for t in (v_both, k_both):
            zeroed.did(pool.memset(f32(t[:]), 0.0))

        PASSES = S // P // RING
        x_here = [Signal(nc, ctx, f"x_here{i}", 1, sp, 16) for i in range(RING)]
        split_hi = Signal(nc, ctx, "gram_hi", RING, act)
        split_lo = Signal(nc, ctx, "gram_lo", RING, dve)
        summed = Signal(nc, ctx, "gram_sum", RING, pool)
        used = Signal(nc, ctx, "gram_mm", RING, pe)

        def gram_load(n):
            for t in range(RING):
                split_lo.wait(sp, n - 1, t + 1)
                summed.wait(sp, n - 1, t + 1)
                stands_alone(sp)
                x_here[t].by(sp.dma_start(x_in[t][:], io["x_rows"][bass.ds((n * RING + t) * P, P), :]))

        def gram_pass(b, n, first, last):
            for t in range(RING):
                x_here[t].wait(act, n, 1)
                used.wait(act, n - 1, t + 1)
                split_hi.by(act.activation(x_hi[t][:], x_in[t][:], ACT.Copy))
                split_hi.wait(dve, n, t + 1)
                used.wait(dve, n - 1, t + 1)
                split_lo.by(dve.tensor_tensor(x_lo[t][:], x_in[t][:], f32(x_hi[t][:]), ALU.subtract))
                x_here[t].wait(pool, n, 1)
                summed.wait(pool, n, t)
                summed.by(pool.tensor_tensor(x_sum[:, b, :], x_sum[:, b, :], x_in[t][:], ALU.add))
                split_lo.wait(pe, n, t + 1)
                for i in range(KT):
                    c0 = min(i * P, D - 2 * P)
                    cols = slice(i * P, (i + 1) * P)
                    m = three_pass(pe, gram[b][i][:, c0:D], (x_hi[t][:, cols], x_lo[t][:, cols]),
                                   (x_hi[t][:, c0:D], x_lo[t][:, c0:D]),
                                   first=first and t == 0, last=last and t == RING - 1)
                used.by(m)

        gram_load(0)
        x_here[0].wait(act, 0, 1)
        loads[0].did(act.dma_start(ctx_t[:], io["ctx_cols"].rearrange("(k p) n -> p k n", p=P)))
        loads[1].did(act.dma_start(w_v[:], io["cross_wv"].rearrange("(k p) n -> p k n", p=P)))
        loads[2].did(act.dma_start(w_k[:], io["cross_wk"].rearrange("(k p) n -> p k n", p=P)))
        loads[3].did(act.dma_start(bv_row[:], io["rows"][3:4, :].broadcast_to([P, D])))
        loads[4].did(act.dma_start(col_sb[:], io["cols"]))
        zeroed.wait(pool, sum_zero)
        gram_pass(0, 0, True, False)

        loads[0].wait(pe)
        loads[1].wait(pe)
        v_ready = []
        for r, (r0, rn) in enumerate(rows_of):
            for k in range(KT):
                m = pe.matmul(gram[1][r][0:rn, :], ctx_t[:, k, r0:r0 + rn], w_v[:, k, :],
                              start=(k == 0), stop=(k == KT - 1))
            v_ready.append(mm.did(m))
        loads[3].wait(dve)
        v_read = []
        for r, (r0, rn) in enumerate(rows_of):
            mm.wait(dve, v_ready[r])
            v_read.append(on_dve.did(dve.tensor_tensor(v_raw[0:rn, r, :], gram[1][r][0:rn, :], bv_row[0:rn, :],
                                                       ALU.add)))
            on_dve.wait(act, v_read[r])
            hi = on_act.did(act.activation(vn_hi[0:rn, r, :], v_raw[0:rn, r, :], ACT.Copy))
            on_act.wait(dve, hi)
            v_done = on_dve.did(dve.tensor_tensor(vn_lo[0:rn, r, :], v_raw[0:rn, r, :],
                                                  f32(vn_hi[0:rn, r, :]), ALU.subtract))
        loads[2].wait(pe)
        loads[4].wait(act)
        loads[4].wait(dve)
        bk = col_sb[:, 3 * KT:4 * KT]
        for m4 in range(KT):
            bank = gram[1][(m4 - 1) % KT]
            if m4:
                on_dve.wait(pe, v_read[m4 - 1])
            for k in range(KT):
                m = pe.matmul(bank[:, 0:B * CTX], w_k[:, k, m4 * P:(m4 + 1) * P], ctx_t[:, k, :],
                              start=(k == 0), stop=(k == KT - 1))
            done = mm.did(m)
            mm.wait(act, done)
            hi = on_act.did(act.activation(kt_hi[:, m4, :], bank[:, 0:B * CTX], ACT.Identity,
                                           bias=bk[:, m4:m4 + 1]))
            on_act.wait(dve, hi)
            k_done = on_dve.did(dve.scalar_tensor_tensor(kt_lo[:, m4, :], bank[:, 0:B * CTX],
                                                         bk[:, m4:m4 + 1], f32(kt_hi[:, m4, :]),
                                                         ALU.add, ALU.subtract))

        def place_v(heads):
            for b in range(B):
                for j in heads:
                    key = 0
                    while key < CTX:
                        row, flat = b * CTX + key, j * CTX + key
                        n = min(CTX - key, P - row % P, P - flat % P)
                        placed.did(sp.dma_start(
                            f32(v_both[flat % P:flat % P + n, b, flat // P])
                            .rearrange("p x g f -> p (x g) f")[:, :, j * DK:(j + 1) * DK],
                            f32(vn[row % P:row % P + n, row // P])
                            .rearrange("p x (g f) -> p (x g) f", g=HG)[:, :, j * DK:(j + 1) * DK]))
                        key += n

        def place_k():
            for b in range(B):
                for j in range(HPG):
                    placed.did(sp.dma_start(f32(k_both[j * DK:(j + 1) * DK, b]).rearrange("p x g n -> p (x g) n")
                                            [:, :, j * CTX:(j + 1) * CTX],
                                            f32(kt[j * DK:(j + 1) * DK]).rearrange("p x k n -> p (x k) n")
                                            [:, :, b * CTX:(b + 1) * CTX]))

        with nc.Fori(1, PASSES - 1) as n:
            gram_load(n)
            gram_pass(0, n, False, False)
        gram_load(PASSES - 1)
        zeroed.wait(sp)
        on_dve.wait(sp, v_done)
        place_v([0])
        gram_pass(0, PASSES - 1, False, True)
        for name, t in fold_w.items():
            weights_in.did(act.dma_start(t[:], io[name].rearrange("(k p) n -> p k n", p=P)))
        gram_load(PASSES)
        place_v([1, 2])
        on_dve.wait(pe, k_done)
        gram_pass(1, PASSES, True, False)
        with nc.Fori(PASSES + 1, 2 * PASSES - 1) as n:
            gram_load(n)
            gram_pass(1, n, False, False)
        gram_load(2 * PASSES - 1)
        place_v([3])
        on_dve.wait(sp, k_done)
        place_k()
        gram_pass(1, 2 * PASSES - 1, False, True)
        placed.wait(sp)
        weights_in.wait(sp)


def fold(nc, io, mem, kv, col_sb, gram, psum8, fold_w, m_out, c_row, w_q_raw):
    from contextlib import ExitStack

    x_sum = kv[4]
    m_hi, m_lo = m_out
    ident, ones = io["ident"], io["ones"]
    sp, act, pe, dve, pool = nc.sync, nc.scalar, nc.tensor, nc.vector, nc.gpsimd
    with ExitStack() as ctx:
        g = mem.place("g_then_u", [P, B, KT, D])
        t = mem.place("t_then_m", [P, B, KT, D])
        kv_t = mem.place("kv_t", [P, B, KT, P])
        rows = mem.place("self_rows", [P, 3, D])
        s_col = mem.place("s_col", [P, B, KT])
        t0_col = mem.place("t0_col", [P, B, KT])
        bq_wide = mem.place("bq_wide", [P, KT, P])

        ctx.enter_context(nc.Block())
        rows_in = Count(nc, ctx, "self_rows_in", 16)
        wq_in = Count(nc, ctx, "cross_wq_in", 16)
        mm = Count(nc, ctx, "fold_mm")
        dv = Count(nc, ctx, "fold_dve")
        ac = Count(nc, ctx, "fold_act")
        pz = Count(nc, ctx, "fold_pool")

        for r in range(3):
            rows_in.did(sp.dma_start(rows[:, r, :], io["rows"][r:r + 1, :].broadcast_to([P, D])))
        wq_in.did(sp.dma_start(w_q_raw[:], io["cross_wq"].rearrange("(k p) n -> p k n", p=P)))
        pz.did(pool.memset(kv_t[:], 0.0))

        g_done = []
        for b in range(B):
            for i in range(KT):
                c0 = min(i * P, D - 2 * P)
                if i % 2:
                    g_done.append((ac, ac.did(act.activation(g[:, b, i, c0:D], gram[b][i][:, c0:D], ACT.Copy))))
                else:
                    g_done.append((dv, dv.did(dve.tensor_copy(g[:, b, i, c0:D], gram[b][i][:, c0:D]))))
        for k in range(KT):
            bq = dv.did(dve.tensor_scalar(bq_wide[:, k, :], ones[:], col_sb[:, k:k + 1], None, ALU.mult))
        lower = [(i, j) for i in range(KT) for j in range(i) if j * P < min(i * P, D - 2 * P)]
        for c, v in g_done:
            c.wait(pe, v)
        small = {}
        for b in range(B):
            for k in range(KT):
                m = pe.matmul(psum8[2 * b][:, k:k + 1], x_sum[:, b, k * P:(k + 1) * P], ones[:, 0:1],
                              start=True, stop=True)
            small[b] = mm.did(m)
        mirrored = {}
        for b in range(B):
            for n, (i, j) in enumerate(lower):
                bank = psum8[2 * b + 1] if n < KT else psum8[4 + b]
                m = pe.transpose(bank[:, (n % KT) * P:(n % KT + 1) * P], g[:, b, j, i * P:(i + 1) * P], ident[:])
            mirrored[b] = mm.did(m)
        g_whole, s_done = {}, {}
        for b in range(B):
            mm.wait(dve, small[b])
            s_done[b] = dv.did(dve.tensor_copy(s_col[:, b, :], psum8[2 * b][:, 0:KT]))
            mm.wait(dve, mirrored[b])
            for n, (i, j) in enumerate(lower):
                bank = psum8[2 * b + 1] if n < KT else psum8[4 + b]
                g_whole[b] = dv.did(dve.tensor_copy(g[:, b, i, j * P:(j + 1) * P],
                                                    bank[:, (n % KT) * P:(n % KT + 1) * P]))

        w_v, w_k, w_o, w_q = (fold_w[n] for n in ("self_wv", "self_wk", "self_wo", "self_wq"))
        rows_in.wait(dve)
        t_done = {}
        last_read = {}
        order = [6, 7, 4, 5, 0, 1, 2, 3]
        turn = [0]

        def next_bank():
            n = order[turn[0] % 8]
            turn[0] += 1
            if n in last_read:
                c, v = last_read[n]
                c.wait(pe, v)
            return n, psum8[n]

        for b in range(B):
            last_read[2 * b] = (dv, s_done[b])
            last_read[2 * b + 1] = last_read[4 + b] = (dv, g_whole[b])
        for b in range(B):
            dv.wait(pe, g_whole[b])
            for i in range(KT):
                n, bank = next_bank()
                for k in range(KT):
                    m = pe.matmul(bank[:], g[:, b, k, i * P:(i + 1) * P], w_v[:, k, :],
                                  start=(k == 0), stop=(k == KT - 1))
                v = mm.did(m)
                mm.wait(dve, v)
                dv.wait(dve, s_done[b])
                t_done[b] = dv.did(dve.scalar_tensor_tensor(t[:, b, i, :], rows[:, 1, :], s_col[:, b, i:i + 1],
                                                            bank[:], ALU.mult, ALU.add))
                last_read[n] = (dv, t_done[b])
        t0_done = {}
        for b in range(B):
            dv.wait(pe, s_done[b])
            n, bank = next_bank()
            for q in range(KT):
                for k in range(KT):
                    m = pe.matmul(bank[:, q:q + 1], w_v[:, k, q * P:(q + 1) * P], s_col[:, b, k:k + 1],
                                  start=(k == 0), stop=(k == KT - 1))
            v = mm.did(m)
            mm.wait(dve, v)
            t0_done[b] = dv.did(dve.scalar_tensor_tensor(t0_col[:, b, :], col_sb[:, KT:2 * KT], float(S),
                                                         bank[:, 0:KT], ALU.mult, ALU.add))
            last_read[n] = (dv, t0_done[b])
        pz.wait(dve)
        kv_done, u_done = {}, {}
        for b in range(B):
            dv.wait(pe, t_done[b])
            n, bank = next_bank()
            for q in range(KT):
                for k in range(KT):
                    m = pe.matmul(bank[:, q * P:(q + 1) * P], t[:, b, k, q * P:(q + 1) * P],
                                  w_k[:, k, q * P:(q + 1) * P], start=(k == 0), stop=(k == KT - 1))
            v = mm.did(m)
            mm.wait(dve, v)
            dv.wait(dve, t0_done[b])
            for q in range(KT):
                for h in range(2):
                    r = slice(h * SELF_DH, (h + 1) * SELF_DH)
                    c = slice(q * P + h * SELF_DH, q * P + (h + 1) * SELF_DH)
                    kv_done[b] = dv.did(dve.scalar_tensor_tensor(
                        kv_t[r, b, q, r], rows[r, 0, c], t0_col[r, b, q:q + 1], bank[r, c], ALU.mult, ALU.add))
            last_read[n] = (dv, kv_done[b])
        for b in range(B):
            dv.wait(pe, kv_done[b])
            for q in range(KT):
                n, bank = next_bank()
                v = mm.did(pe.matmul(bank[:], kv_t[:, b, q, :], w_o[:, q, :], start=True, stop=True))
                mm.wait(act, v)
                u_done[b] = ac.did(act.activation(g[:, b, q, :], bank[:], ACT.Copy))
                last_read[n] = (ac, u_done[b])
        for b in range(B):
            ac.wait(pe, u_done[b])
            dv.wait(pe, bq)
            n, bank = next_bank()
            for q in range(KT):
                m = pe.matmul(bank[:], bq_wide[:, q, :], g[:, b, q, :], start=(q == 0), stop=(q == KT - 1))
            v = mm.did(m)
            mm.wait(dve, v)
            last_read[n] = (dv, dv.did(dve.tensor_tensor(c_row[:, b, :], bank[:], rows[:, 2, :], ALU.add)))
        for b in range(B):
            for i in range(KT):
                n, bank = next_bank()
                for q in range(KT):
                    m = pe.matmul(bank[:], w_q[:, q, i * P:(i + 1) * P], g[:, b, q, :],
                                  start=(q == 0), stop=(q == KT - 1))
                v = mm.did(m)
                mm.wait(act, v)
                copied = ac.did(act.activation(t[:, b, i, :], bank[:], ACT.Copy))
                last_read[n] = (ac, copied)
                ac.wait(dve, copied)
                eye = dv.did(dve.tensor_tensor(t[:, b, i, i * P:(i + 1) * P], t[:, b, i, i * P:(i + 1) * P],
                                               ident[:], ALU.add))
                dv.wait(act, eye)
                hi = ac.did(act.activation(m_hi[:, b, i, :], t[:, b, i, :], ACT.Copy))
                ac.wait(dve, hi)
                dv.did(dve.tensor_tensor(m_lo[:, b, i, :], t[:, b, i, :], f32(m_hi[:, b, i, :]), ALU.subtract))
        wq_in.wait(sp)


def attend(nc, io, mem, kv, col_sb, psum, m_in, c_row, w_q_raw, scratch):
    from contextlib import ExitStack

    k_hi, k_lo, v_hi, v_lo = kv[:4]
    m_hi, m_lo = m_in
    ident = io["ident"]
    x1_dram, o_dram = scratch
    sp, act, pe, dve, pool = nc.sync, nc.scalar, nc.tensor, nc.vector, nc.gpsimd
    BUFS = 4
    LEAD = 3
    VALUES_AT = (2, 4, 5, 7)
    with ExitStack() as ctx:
        wq_hi, wq_lo = mem.pair("cross_wq", [P, KT, D])
        x_in = mem.place("x_cols_in", [P, KT, GT])
        xt_hi, xt_lo = mem.pair("xt", [P, KT, GT])
        x1 = mem.place("x1", [P, TPG, D])
        x1t_hi, x1t_lo = mem.pair("x1t", [P, KT, GT])
        q_hi, q_lo = mem.pair("q", [P, HG, GT])
        prob = [mem.place(f"prob{i}", [P, CH * P]) for i in range(BUFS)]
        out_t = mem.place("out_t", [P, HG, GT])
        mask_in = mem.place("mask_in", [P, TPG, CTX], I32)
        mask_add = [mem.place(f"mask_add{i}", [P, TPG, CTX]) for i in range(B)]
        stats = mem.place("stats", [P, TPG, 6])
        moments = mem.place("moments", [P, TPG, 2])
        var_eps = mem.place("var_eps", [P, TPG])
        rstd = mem.place("rstd", [P, TPG])
        neg_half = mem.place("neg_half", [P, TPG])
        row_min = mem.place("row_min", [P, BUFS, HPG])
        row_sum = mem.place("row_sum", [P, BUFS, HPG])
        row_inv = mem.place("row_inv", [P, BUFS, HPG])
        assert mem.at <= mem.end - 4 * CH * GT * 4, (mem.at, mem.end)
        mem.at = mem.end - 4 * CH * GT * 4
        pt = [mem.pair(f"prob_t{i}", [P, CH, GT]) for i in range(2)]

        ctx.enter_context(nc.Block())
        setup = Count(nc, ctx, "attend_constants")
        w_hi_ok, w_lo_ok = Count(nc, ctx, "wq_hi_ok"), Count(nc, ctx, "wq_lo_ok")
        alone = ctx.enter_context(nc.semaphore("alone_attend"))
        sig = lambda name, per, eng, step=1: Signal(nc, ctx, name, per, eng, step)
        x_here = sig("x_here", 1, sp, 16)
        x_hi_ok, x_lo_ok = sig("x_hi_ok", 1, act), sig("x_lo_ok", 1, pool)
        y_mm, y_read = sig("y_mm", TPG, pe), sig("y_read", TPG, dve)
        y_stat, y_mom = sig("y_stat", TPG, dve), sig("y_mom", TPG, dve)
        y_var, y_rstd = sig("y_var", 1, dve), sig("y_rstd", 1, pool)
        x1_ok, x1_kept = sig("x1_ok", TPG, dve), sig("x1_kept", 1, sp, 16)
        tr_mm, x1t_hi_ok, x1t_lo_ok = sig("tr_mm", TPG, pe), sig("x1t_hi_ok", TPG, act), sig("x1t_lo_ok", TPG, dve)
        q_mm, q_hi_ok, q_lo_ok = sig("q_mm", 2, pe), sig("q_hi_ok", 2, act), sig("q_lo_ok", 2, dve)
        mask_here, mask_ok = sig("mask_here", 1, sp, 16), sig("mask_ok", 1, dve)
        s_mm, s_min = sig("s_mm", UNITS, pe), sig("s_min", UNITS, dve)
        p_exp, p_inv, p_norm = sig("p_exp", UNITS, act), sig("p_inv", UNITS, dve), sig("p_norm", UNITS, pool)
        t_mm, t_hi_ok, t_lo_ok = sig("t_mm", UNITS, pe), sig("t_hi_ok", UNITS, act), sig("t_lo_ok", UNITS, dve)
        pv_mm, o_read = sig("pv_mm", HG, pe), sig("o_read", HG, act)
        o_kept = sig("o_kept", 1, sp, 16)

        def stands_alone(engine):
            engine.sem_inc(alone, 1)

        def token0(b, j):
            return j * GT + b * S

        for t in prob:
            setup.did(pool.memset(t[:, GK:CH * P], 0.0))
        pad_ok = setup.did(pool.memset(neg_half[:], -0.5))
        setup.wait(dve, pad_ok)
        w_hi_ok.did(act.activation(wq_hi[:], w_q_raw[:], ACT.Copy))
        w_hi_ok.wait(dve)
        w_lo_ok.did(dve.tensor_tensor(wq_lo[:], w_q_raw[:], f32(wq_hi[:]), ALU.subtract))
        w_lo_ok.wait(pe)
        setup.wait(pool, pad_ok)

        def load_x(n, b, j):
            x_hi_ok.wait(sp, n - 1, 1)
            x_lo_ok.wait(sp, n - 1, 1)
            stands_alone(sp)
            x_here.by(sp.dma_start(x_in[:], io["x_cols"].rearrange("(k p) n -> p k n", p=P)
                                   [:, :, bass.ds(token0(b, j), GT)]))

        def load_mask(n, b, j):
            mask_ok.wait(sp, n - 1, 1)
            stands_alone(sp)
            mask_here.by(sp.dma_start(mask_in[:], io["mask"][bass.ds(token0(b, j), GT), :]
                                      .rearrange("(t p) c -> p t c", p=P)))

        def split_x(n):
            x_here.wait(act, n, 1)
            y_mm.wait(act, n - 1, TPG)
            x_hi_ok.by(act.activation(xt_hi[:], x_in[:], ACT.Copy))
            x_hi_ok.wait(pool, n, 1)
            y_mm.wait(pool, n - 1, TPG)
            x_lo_ok.by(pool.tensor_tensor(xt_lo[:], x_in[:], f32(xt_hi[:]), ALU.subtract))

        def make_mask(n, b):
            mask_here.wait(dve, n, 1)
            if not (isinstance(n, int) and n == 0):
                s_min.wait(dve, n - B, UNITS)
            mask_ok.by(dve.tensor_scalar(mask_add[b][:], mask_in[:], 0.0, NEG, ALU.is_equal, ALU.mult))

        def y_product(n, b, t):
            if t == 0:
                q_lo_ok.wait(pe, n - 1, 2)
                x_hi_ok.wait(pe, n, 1)
                x_lo_ok.wait(pe, n, 1)
            else:
                y_read.wait(pe, n, t)
            for k in range(KT):
                cols = slice(t * P, (t + 1) * P)
                m = three_pass(pe, psum["next"][:], (xt_hi[:, k, cols], xt_lo[:, k, cols]),
                               (m_hi[:, b, k, :], m_lo[:, b, k, :]), first=(k == 0), last=(k == KT - 1))
            y_mm.by(m)

        def y_finish(n, b, t):
            y_mm.wait(dve, n, t + 1)
            if t == 0:
                tr_mm.wait(dve, n - 1, TPG)
                x1_kept.wait(dve, n - 1, 1)
            y_read.by(dve.tensor_tensor(x1[:, t, :], psum["next"][:], c_row[:, b, :], ALU.add))
            y_read.wait(dve, n, t + 1)
            y_stat.by(dve.bn_stats(stats[:, t, :], x1[:, t, :]))
            y_stat.wait(dve, n, t + 1)
            stands_alone(dve)
            y_mom.by(dve.bn_aggr(moments[:, t, :], stats[:, t, :]))
            if t == TPG - 1:
                y_mom.wait(dve, n, TPG)
                y_rstd.wait(dve, n - 1, 1)
                y_var.by(dve.tensor_scalar(var_eps[:], moments[:, :, 1], EPS, None, ALU.add))
                y_var.wait(pool, n, 1)
                x1_ok.wait(pool, n - 1, TPG)
                y_rstd.by(pool.tensor_tensor(rstd[:], var_eps[:], neg_half[:], ALU.pow))

        def x1_finish(n, b, j):
            y_rstd.wait(dve, n, 1)
            for t in range(TPG):
                x1_ok.by(dve.tensor_scalar(x1[:, t, :], x1[:, t, :], moments[:, t, 0:1], rstd[:, t:t + 1],
                                           ALU.subtract, ALU.mult))
            x1_ok.wait(sp, n, TPG)
            stands_alone(sp)
            x1_kept.by(sp.dma_start(x1_dram[bass.ds(token0(b, j), GT), :].rearrange("(t p) d -> p t d", p=P), x1[:]))

        def x1_transpose(n, t):
            bank = psum["next"] if t == 0 else psum["value"]
            x1_ok.wait(pe, n, t + 1)
            if t == 0:
                y_read.wait(pe, n, TPG)
            else:
                o_read.wait(pe, n - 1, 1)
            for k in range(KT):
                m = pe.transpose(bank[:, k * P:(k + 1) * P], x1[:, t, k * P:(k + 1) * P], ident[:])
            tr_mm.by(m)

        def x1t_split(n, t):
            bank = (psum["next"] if t == 0 else psum["value"])[:].rearrange("p (k n) -> p k n", k=KT)
            cols = slice(t * P, (t + 1) * P)
            tr_mm.wait(act, n, t + 1)
            q_mm.wait(act, n - 1, 2)
            x1t_hi_ok.by(act.activation(x1t_hi[:, :, cols], bank, ACT.Copy))
            x1t_hi_ok.wait(dve, n, t + 1)
            x1t_lo_ok.by(dve.tensor_tensor(x1t_lo[:, :, cols], bank, f32(x1t_hi[:, :, cols]), ALU.subtract))

        def q_product(n, h):
            if h == 0:
                x1t_lo_ok.wait(pe, n, TPG)
            else:
                q_lo_ok.wait(pe, n, h)
            for i in range(2):
                cols = slice((2 * h + i) * P, (2 * h + i + 1) * P)
                for k in range(KT):
                    m = three_pass(pe, psum["next"][:, i * GT:(i + 1) * GT], (wq_hi[:, k, cols], wq_lo[:, k, cols]),
                                   (x1t_hi[:, k, :], x1t_lo[:, k, :]), first=(k == 0), last=(k == KT - 1))
            q_mm.by(m)

        def q_split(n, h):
            q_mm.wait(act, n, h + 1)
            s_mm.wait(act, n - 1, UNITS * (h + 1) // 2)
            bq = col_sb[:, 2 * KT:3 * KT]
            for i in range(2):
                g = 2 * h + i
                m = act.activation(q_hi[:, g, :], psum["next"][:, i * GT:(i + 1) * GT], ACT.Identity,
                                   bias=bq[:, g:g + 1])
            q_hi_ok.by(m)
            q_hi_ok.wait(dve, n, h + 1)
            for i in range(2):
                g = 2 * h + i
                m = dve.scalar_tensor_tensor(q_lo[:, g, :], psum["next"][:, i * GT:(i + 1) * GT], bq[:, g:g + 1],
                                             f32(q_hi[:, g, :]), ALU.add, ALU.subtract)
            q_lo_ok.by(m)

        def scores(n, b, u):
            g, t = divmod(u, TPG)
            bank = psum["scores"][u % 2]
            if u % (UNITS // 2) == 0:
                q_lo_ok.wait(pe, n, 1 + u // (UNITS // 2))
            s_min.wait(pe, n, u - 1)
            cols = slice(t * P, (t + 1) * P)
            for sta, mov, first, last in ((q_hi, k_hi, True, False), (q_hi, k_lo, False, False), (q_lo, k_hi, False, True)):
                for h in range(2):
                    m = pe.matmul(bank[:, h, 0:HALF], sta[:, g, cols], mov[:, b, g, h * HALF:(h + 1) * HALF],
                                  start=first, stop=last, skip_group_check=True)
            s_mm.by(m)

        def masked_min(n, b, u):
            t, buf = u % TPG, u % BUFS
            if u == 0:
                mask_ok.wait(dve, n, 1)
            s_mm.wait(dve, n, u + 1)
            t_mm.wait(dve, n, u + 1 - BUFS)
            stands_alone(dve)
            for h in range(HPG):
                m = dve.tensor_tensor_reduce(prob[buf][:, h * CTX:(h + 1) * CTX],
                                             psum["scores"][u % 2][:, h // 2, (h % 2) * CTX:(h % 2 + 1) * CTX],
                                             mask_add[b][:, t, :], -SCALE, HUGE, ALU.add, ALU.min,
                                             row_min[:, buf, h:h + 1])
            s_min.by(m)

        def exponentials(n, u):
            buf = u % BUFS
            s_min.wait(act, n, u + 1)
            for h in range(HPG):
                keys = prob[buf][:, h * CTX:(h + 1) * CTX]
                m = act.activation(keys, keys, ACT.Exp, bias=row_min[:, buf, h:h + 1], scale=-1.0,
                                   accum_out=row_sum[:, buf, h:h + 1])
            p_exp.by(m)

        def normalise(n, u):
            buf = u % BUFS
            p_exp.wait(dve, n, u + 1)
            p_inv.by(dve.reciprocal(row_inv[:, buf, :], row_sum[:, buf, :]))
            keys = prob[buf][:, 0:GK].rearrange("p (h c) -> p h c", h=HPG)
            p_inv.wait(pool, n, u + 1)
            p_norm.by(pool.tensor_tensor(keys, keys, row_inv[:, buf, :].unsqueeze(2).broadcast_to([P, HPG, CTX]),
                                         ALU.mult))

        def transposes(n, u):
            p_norm.wait(pe, n, u + 1)
            t_lo_ok.wait(pe, n, u)
            for c in range(CH):
                m = pe.transpose(psum["turned"][:, c * P:(c + 1) * P], prob[u % BUFS][:, c * P:(c + 1) * P], ident[:])
            t_mm.by(m)

        def transposed_split(n, u):
            g, t = divmod(u, TPG)
            hi, lo = (x[:, :, t * P:(t + 1) * P] for x in pt[g % 2])
            src = psum["turned"][:, 0:CH * P].rearrange("p (c n) -> p c n", c=CH)
            t_mm.wait(act, n, u + 1)
            pv_mm.wait(act, n, g - 1)
            t_hi_ok.by(act.activation(hi, src, ACT.Copy))
            t_hi_ok.wait(dve, n, u + 1)
            t_lo_ok.by(dve.tensor_tensor(lo, src, f32(hi), ALU.subtract))

        def values(n, b, g, next_group):
            t_lo_ok.wait(pe, n, (g + 1) * TPG)
            o_read.wait(pe, n, g)
            if g == 1 and next_group:
                x1t_lo_ok.wait(pe, n + 1, TPG)
            hi, lo = pt[g % 2]
            for c in range(CH):
                m = three_pass(pe, psum["value"][:, 0:GT], (v_hi[:, b, c, g, :], v_lo[:, b, c, g, :]),
                               (hi[:, c, :], lo[:, c, :]), first=(c == 0), last=(c == CH - 1))
            pv_mm.by(m)
            pv_mm.wait(act, n, g + 1)
            if g == 0:
                o_kept.wait(act, n - 1, 1)
            o_read.by(act.activation(out_t[:, g, :], psum["value"][:, 0:GT], ACT.Copy))

        def store_values(n, b, j):
            o_read.wait(sp, n, HG)
            stands_alone(sp)
            o_kept.by(sp.dma_start(o_dram.rearrange("(g p) n -> p g n", p=P)[:, :, bass.ds(token0(b, j), GT)], out_t[:]))

        def unit(n, b, u, ahead):
            if u < UNITS:
                return n, b, u
            return (n + 1, (b + 1) % B, u - UNITS) if ahead else None

        def step(n, b, j, u, ahead, ahead2):
            b1, j1 = (b + 1) % B, j + (b + 1) // B
            transposes(n, u)
            if ahead:
                if u == 1:
                    y_finish(n + 1, b1, 0)
                if u == 2:
                    y_finish(n + 1, b1, 1)
                if u == 7:
                    q_split(n + 1, 1)
            transposed_split(n, u)
            if u + LEAD == UNITS and ahead:
                make_mask(n + 1, b1)
            if (x := unit(n, b, u + LEAD, ahead)) is not None:
                scores(*x)
                masked_min(*x)
            if (x := unit(n, b, u + LEAD - 1, ahead)) is not None:
                exponentials(x[0], x[2])
                normalise(x[0], x[2])
            if u == 2 and ahead:
                x1_finish(n + 1, b1, j1)
            if ahead:
                if u < TPG:
                    y_product(n + 1, b1, u)
                if u == 3:
                    x1_transpose(n + 1, 0)
                    x1_transpose(n + 1, 1)
                    x1t_split(n + 1, 0)
                    x1t_split(n + 1, 1)
                if u == 4:
                    q_product(n + 1, 0)
                    q_split(n + 1, 0)
                if u == 6:
                    q_product(n + 1, 1)
            if u in VALUES_AT:
                values(n, b, VALUES_AT.index(u), ahead)
            if u == 3 and ahead2:
                split_x(n + 2)
            if u == UNITS - 1:
                store_values(n, b, j)

        def group(n, b, j, ahead, ahead2):
            b1, j1 = (b + 1) % B, j + (b + 1) // B
            if ahead:
                load_mask(n + 1, b1, j1)
            if ahead2:
                load_x(n + 2, b, j + 1)
            for u in range(UNITS):
                step(n, b, j, u, ahead, ahead2)

        load_mask(0, 0, 0)
        load_x(0, 0, 0)
        split_x(0)
        load_x(1, 1, 0)
        make_mask(0, 0)
        for t in range(TPG):
            y_product(0, 0, t)
            y_finish(0, 0, t)
        split_x(1)
        x1_finish(0, 0, 0)
        for t in range(TPG):
            x1_transpose(0, t)
            x1t_split(0, t)
        for h in range(2):
            q_product(0, h)
            q_split(0, h)
        for u in range(LEAD):
            scores(0, 0, u)
            masked_min(0, 0, u)
            if u < LEAD - 1:
                exponentials(0, u)
                normalise(0, u)
        with nc.Fori(0, NG // B - 1) as j:
            for b in range(B):
                group(B * j + b, b, j, True, True)
        last = NG // B - 1
        for b in range(B):
            group(B * last + b, b, last, b < B - 1, False)
        x1_kept.wait(sp, NG - 1, 1)
        o_kept.wait(sp, NG - 1, 1)


def feed(nc, io, mem, col_sb, psum8, scratch, out):
    from contextlib import ExitStack

    ident = io["ident"]
    x1_dram, o_dram = scratch
    sp, act, pe, dve, pool = nc.sync, nc.scalar, nc.tensor, nc.vector, nc.gpsimd
    o_bank, tr_bank, k_bank, rv_bank = psum8[0:2], psum8[2:4], psum8[4:6], psum8[6:8]
    with ExitStack() as ctx:
        names = ("cross_wo", "ffn_wk", "ffn_wr", "ffn_wv")
        raw = {w: mem.place(w + "_raw", [P, KT, D]) for w in names}
        w = {x: mem.pair(x, [P, KT, D]) for x in names}
        bo_row = mem.place("cross_bo_row", [P, D])
        o_in = mem.place("o_in", [P, HG, GT])
        ot = mem.pair("o_t", [P, HG, GT])
        x1_in = mem.place("x1_in", [P, TPG, D])
        x2 = [mem.place(f"x2_{b}", [P, TPG, D]) for b in range(B)]
        x2t = [mem.place(f"x2_t{b}", [P, KT, 1 + GT]) for b in range(B)]
        diff = mem.place("diff", [P, KT, GT])
        mixed = {g: mem.place("mixed_" + g, [P, KT, GT]) for g in "kr"}
        mix = {g: mem.pair("mix_" + g, [P, KT, GT]) for g in "kr"}
        relu = mem.place("relu", [P, KT, GT])
        square = mem.place("square", [P, KT, GT])
        ka = mem.pair("k_act", [P, KT, GT])
        gate = mem.place("gate", [P, TPG, D])
        y3 = mem.place("y3", [P, TPG, D])
        neg_half = mem.place("neg_half4", [P, TPG])
        norm = {k: (mem.place(f"stats_{k}", [P, TPG, 6]), mem.place(f"moments_{k}", [P, TPG, 2]),
                    mem.place(f"var_{k}", [P, TPG]), mem.place(f"rstd_{k}", [P, TPG])) for k in (2, 3)}

        ctx.enter_context(nc.Block())
        setup = [Count(nc, ctx, f"feed_load{i}", 16) for i in range(5)]
        ready = Count(nc, ctx, "feed_constants")
        w_hi_ok, w_lo_ok = Count(nc, ctx, "feed_w_hi"), Count(nc, ctx, "feed_w_lo")
        alone = ctx.enter_context(nc.semaphore("alone_feed"))
        sig = lambda name, per, eng, step=1: Signal(nc, ctx, name, per, eng, step)
        o_here, x1_here, x1_bo = sig("o_here", 1, sp, 16), sig("x1_here", 1, sp, 16), sig("x1_bo", 1, pool)
        ot_hi_ok, ot_lo_ok = sig("ot_hi_ok", 1, act), sig("ot_lo_ok", 1, pool)
        o_mm, o_read = sig("o_mm", TPG, pe), sig("o_read4", TPG, dve)
        ln = {k: dict(stat=sig(f"stat{k}", TPG, dve), mom=sig(f"mom{k}", TPG, dve), var=sig(f"var{k}", 1, dve),
                      rstd=sig(f"rstd{k}", 1, pool), done=sig(f"ln{k}", TPG, dve)) for k in (2, 3)}
        tr_mm, tr_read = sig("tr_mm4", TPG, pe), sig("tr_read", TPG, act)
        carried, diff_ok = sig("carried", 1, dve), sig("diff_ok", 1, dve)
        mix_ok = {g: sig("mixed_ok_" + g, 1, dve) for g in "kr"}
        mix_hi = {g: sig("mix_hi_" + g, 1, act) for g in "kr"}
        mix_lo = {"k": sig("mix_lo_k", 1, dve), "r": sig("mix_lo_r", 1, pool)}
        k_mm, k_relu, k_sq = sig("k_mm", 2, pe), sig("k_relu", 2, act), sig("k_sq", 2, dve)
        ka_hi, ka_lo = sig("ka_hi", 2, act), sig("ka_lo", 2, dve)
        r_mm, r_read = sig("r_mm", TPG, pe), sig("r_read", TPG, act)
        v_mm, v_read, v_sum = sig("v_mm", TPG, pe), sig("v_read", TPG, dve), sig("v_sum", TPG, dve)
        out_kept = sig("out_kept", 1, sp, 16)

        def stands_alone(engine):
            engine.sem_inc(alone, 1)

        def token0(b, j):
            return j * GT + b * S

        def load(n, b, j):
            ot_lo_ok.wait(sp, n - 1, 1)
            stands_alone(sp)
            o_here.by(sp.dma_start(o_in[:], o_dram.rearrange("(g p) n -> p g n", p=P)[:, :, bass.ds(token0(b, j), GT)]))
            o_read.wait(sp, n - 1, TPG)
            stands_alone(sp)
            x1_here.by(sp.dma_start(x1_in[:], x1_dram[bass.ds(token0(b, j), GT), :].rearrange("(t p) d -> p t d", p=P)))

        def take_in(n):
            o_here.wait(act, n, 1)
            o_mm.wait(act, n - 1, TPG)
            ot_hi_ok.by(act.activation(ot[0][:], o_in[:], ACT.Copy))
            ot_hi_ok.wait(pool, n, 1)
            o_mm.wait(pool, n - 1, TPG)
            ot_lo_ok.by(pool.tensor_tensor(ot[1][:], o_in[:], f32(ot[0][:]), ALU.subtract))

        def add_bias(n):
            x1_here.wait(pool, n, 1)
            x1_bo.by(pool.tensor_tensor(x1_in[:], x1_in[:], bo_row[:].unsqueeze(1).broadcast_to([P, TPG, D]), ALU.add))

        def row_product(bank, sta, weight, t):
            cols = slice(t * P, (t + 1) * P)
            for k in range(KT):
                m = three_pass(pe, bank[:], (sta[0][:, k, cols], sta[1][:, k, cols]),
                               (w[weight][0][:, k, :], w[weight][1][:, k, :]), first=(k == 0), last=(k == KT - 1))
            return m

        def moments(key, n, t, rows):
            st, mo, var, rs = norm[key]
            s = ln[key]
            s["stat"].by(dve.bn_stats(st[:, t, :], rows[:, t, :]))
            s["stat"].wait(dve, n, t + 1)
            stands_alone(dve)
            s["mom"].by(dve.bn_aggr(mo[:, t, :], st[:, t, :]))
            if t == TPG - 1:
                s["mom"].wait(dve, n, TPG)
                s["rstd"].wait(dve, n - 1, 1)
                s["var"].by(dve.tensor_scalar(var[:], mo[:, :, 1], EPS, None, ALU.add))
                s["var"].wait(pool, n, 1)
                s["done"].wait(pool, n - 1, TPG)
                s["rstd"].by(pool.tensor_tensor(rs[:], var[:], neg_half[:], ALU.pow))

        def normalise(key, n, rows):
            _, mo, _, rs = norm[key]
            ln[key]["rstd"].wait(dve, n, 1)
            for t in range(TPG):
                ln[key]["done"].by(dve.tensor_scalar(rows[:, t, :], rows[:, t, :], mo[:, t, 0:1], rs[:, t:t + 1],
                                                     ALU.subtract, ALU.mult))

        def o_product(n, t):
            ot_lo_ok.wait(pe, n, 1)
            o_read.wait(pe, n - 1, t + 1)
            o_mm.by(row_product(o_bank[t], ot, "cross_wo", t))

        def o_finish(n, b, t):
            o_mm.wait(dve, n, t + 1)
            x1_bo.wait(dve, n, 1)
            if t == 0 and not (isinstance(n, int) and n < B):
                tr_mm.wait(dve, n - B, TPG)
                v_sum.wait(dve, n - B, TPG)
            o_read.by(dve.tensor_tensor(x2[b][:, t, :], o_bank[t][:], x1_in[:, t, :], ALU.add))
            o_read.wait(dve, n, t + 1)
            moments(2, n, t, x2[b])

        def turn(n, b, t):
            ln[2]["done"].wait(pe, n, t + 1)
            tr_read.wait(pe, n - 1, t + 1)
            for k in range(KT):
                m = pe.transpose(tr_bank[t][:, k * P:(k + 1) * P], x2[b][:, t, k * P:(k + 1) * P], ident[:])
            tr_mm.by(m)

        def turned(n, b, t):
            tr_mm.wait(act, n, t + 1)
            carried.wait(act, n, 1)
            tr_read.by(act.activation(x2t[b][:, :, 1 + t * P:1 + (t + 1) * P],
                                      tr_bank[t][:].rearrange("p (k n) -> p k n", k=KT), ACT.Copy))

        def carry(n, b):
            mix_ok["r"].wait(dve, n - 1, 1)
            carried.by(dve.tensor_copy(x2t[b][:, :, 0:1], x2t[b][:, :, GT:GT + 1]))

        def blend(n, b, g):
            now, before = x2t[b][:, :, 1:1 + GT], x2t[b][:, :, 0:GT]
            if g == "k":
                tr_read.wait(dve, n, TPG)
                mix_ok["r"].wait(dve, n - 1, 1)
                diff_ok.by(dve.tensor_tensor(diff[:], now, before, ALU.subtract))
                diff_ok.wait(dve, n, 1)
            mix_lo[g].wait(dve, n - 1, 1)
            c0 = {"k": 5 * KT, "r": 4 * KT}[g]
            for k in range(KT):
                m = dve.scalar_tensor_tensor(mixed[g][:, k, :], diff[:, k, :], col_sb[:, c0 + k:c0 + k + 1],
                                             before[:, k, :], ALU.mult, ALU.add)
            mix_ok[g].by(m)
            mix_ok[g].wait(act, n, 1)
            last_mm = (k_mm, 2) if g == "k" else (r_mm, TPG)
            last_mm[0].wait(act, n - 1, last_mm[1])
            mix_hi[g].by(act.activation(mix[g][0][:], mixed[g][:], ACT.Copy))

        def blend_low(n, g):
            eng = dve if g == "k" else pool
            mix_hi[g].wait(eng, n, 1)
            mix_lo[g].by(eng.tensor_tensor(mix[g][1][:], mixed[g][:], f32(mix[g][0][:]), ALU.subtract))

        def k_product(n, h):
            mix_lo["k"].wait(pe, n, 1)
            k_sq.wait(pe, n - 1, h + 1)
            for i in range(2):
                cols = slice((2 * h + i) * P, (2 * h + i + 1) * P)
                for k in range(KT):
                    m = three_pass(pe, k_bank[h][:, i * GT:(i + 1) * GT],
                                   (w["ffn_wk"][0][:, k, cols], w["ffn_wk"][1][:, k, cols]),
                                   (mix["k"][0][:, k, :], mix["k"][1][:, k, :]), first=(k == 0), last=(k == KT - 1))
            k_mm.by(m)

        def k_finish(n, h):
            kt = slice(2 * h, 2 * h + 2)
            bank = k_bank[h][:].rearrange("p (k n) -> p k n", k=2)
            k_mm.wait(act, n, h + 1)
            k_sq.wait(act, n - 1, h + 1)
            k_relu.by(act.activation(relu[:, kt, :], bank, ACT.Relu))
            k_relu.wait(dve, n, h + 1)
            ka_lo.wait(dve, n - 1, h + 1)
            k_sq.by(dve.scalar_tensor_tensor(square[:, kt, :], bank, 0.0, relu[:, kt, :], ALU.max, ALU.mult))
            k_sq.wait(act, n, h + 1)
            v_mm.wait(act, n - 1, TPG)
            ka_hi.by(act.activation(ka[0][:, kt, :], square[:, kt, :], ACT.Copy))
            ka_hi.wait(dve, n, h + 1)
            ka_lo.by(dve.tensor_tensor(ka[1][:, kt, :], square[:, kt, :], f32(ka[0][:, kt, :]), ALU.subtract))

        def r_product(n, t):
            mix_lo["r"].wait(pe, n, 1)
            v_read.wait(pe, n - 1, t + 1)
            r_mm.by(row_product(rv_bank[t], mix["r"], "ffn_wr", t))

        def r_gate(n, t):
            r_mm.wait(act, n, t + 1)
            v_read.wait(act, n - 1, t + 1)
            r_read.by(act.activation(gate[:, t, :], rv_bank[t][:], ACT.Tanh, scale=0.5))

        def v_product(n, t):
            ka_lo.wait(pe, n, 2)
            r_read.wait(pe, n, t + 1)
            v_mm.by(row_product(rv_bank[t], ka, "ffn_wv", t))

        def v_finish(n, b, t):
            v_mm.wait(dve, n, t + 1)
            if t == 0:
                out_kept.wait(dve, n - 1, 1)
            v_read.by(dve.scalar_tensor_tensor(y3[:, t, :], gate[:, t, :], 1.0, rv_bank[t][:], ALU.add, ALU.mult))
            v_read.wait(dve, n, t + 1)
            v_sum.by(dve.scalar_tensor_tensor(y3[:, t, :], y3[:, t, :], 0.5, x2[b][:, t, :], ALU.mult, ALU.add))
            v_sum.wait(dve, n, t + 1)
            moments(3, n, t, y3)

        def store(n, b, j):
            ln[3]["done"].wait(sp, n, TPG)
            stands_alone(sp)
            out_kept.by(sp.dma_start(out[bass.ds(token0(b, j), GT), :].rearrange("(t p) d -> p t d", p=P), y3[:]))

        def group(n, b, j, ahead, ahead2):
            b1 = (b + 1) % B
            k_product(n, 0)
            k_finish(n, 0)
            if ahead:
                for t in range(TPG):
                    o_product(n + 1, t)
                    o_finish(n + 1, b1, t)
            if ahead2:
                load(n + 2, b, j + 1)
            k_product(n, 1)
            if ahead:
                normalise(2, n + 1, x2[b1])
                carry(n + 1, b1)
            k_finish(n, 1)
            r_product(n, 0)
            if ahead:
                for t in range(TPG):
                    turn(n + 1, b1, t)
                    turned(n + 1, b1, t)
            r_gate(n, 0)
            r_product(n, 1)
            if ahead2:
                take_in(n + 2)
                add_bias(n + 2)
            r_gate(n, 1)
            if ahead:
                blend(n + 1, b1, "k")
            v_product(n, 0)
            v_finish(n, b, 0)
            if ahead:
                blend_low(n + 1, "k")
            v_product(n, 1)
            v_finish(n, b, 1)
            if ahead:
                blend(n + 1, b1, "r")
                blend_low(n + 1, "r")
            normalise(3, n, y3)
            store(n, b, j)

        for i, name in enumerate(names):
            setup[i].did((sp if i % 2 else act).dma_start(raw[name][:], io[name].rearrange("(k p) n -> p k n", p=P)))
        setup[4].did(act.dma_start(bo_row[:], io["rows"][4:5, :].broadcast_to([P, D])))
        for b in range(B):
            zero = ready.did(pool.memset(x2t[b][:], 0.0))
        zero = ready.did(pool.memset(neg_half[:], -0.5))
        ready.wait(dve, zero)
        ready.wait(pool, zero)
        setup[4].wait(pool)
        load(0, 0, 0)
        take_in(0)
        add_bias(0)

        def split_weight(i):
            name = names[i]
            setup[i].wait(act)
            w_hi_ok.did(act.activation(w[name][0][:], raw[name][:], ACT.Copy))
            w_hi_ok.wait(dve)
            w_lo_ok.did(dve.tensor_tensor(w[name][1][:], raw[name][:], f32(w[name][0][:]), ALU.subtract))
            w_lo_ok.wait(pe)

        split_weight(0)
        for t in range(TPG):
            o_product(0, t)
            o_finish(0, 0, t)
        load(1, 1, 0)
        normalise(2, 0, x2[0])
        carry(0, 0)
        for t in range(TPG):
            turn(0, 0, t)
            turned(0, 0, t)
        for g in "kr":
            blend(0, 0, g)
            blend_low(0, g)
        take_in(1)
        for i in range(1, 4):
            split_weight(i)
        add_bias(1)
        with nc.Fori(0, NG // B - 1) as j:
            for b in range(B):
                group(B * j + b, b, j, True, True)
        last = NG // B - 1
        for b in range(B):
            group(B * last + b, b, last, b < B - 1, False)
        out_kept.wait(sp, NG - 1, 1)


def decoder_layer(nc, io, out):
    from contextlib import ExitStack

    x1_dram = nc.dram_tensor("x1_scratch", (B * S, D), F32, kind="Internal").ap()
    o_dram = nc.dram_tensor("o_scratch", (D, B * S), F32, kind="Internal").ap()
    mem = Map(nc)
    pool, dve = nc.gpsimd, nc.vector
    ident = mem.place("ident", [P, P])
    ones = mem.place("ones", [P, P])
    col_sb = mem.place("cols", [P, len(COLS) * KT])
    keep = mem.at
    k_both, k_hi, k_lo = mem.joined_pair("k_blocks", [P, B, HG, GK], 2)
    v_both, v_hi, v_lo = mem.joined_pair("v_blocks", [P, B, CH, HG, P], 3)
    c_row = mem.place("c_row", [P, B, D])
    kept_kv = mem.at
    x_sum = mem.place("x_sum", [P, B, D])
    fold_w = {n: mem.place(n, [P, KT, D]) for n in ("self_wv", "self_wk", "self_wo", "self_wq")}
    kept_fold = mem.at
    kv = (k_hi, k_lo, v_hi, v_lo, x_sum, k_both, v_both)

    with ExitStack() as ctx:
        made = Count(nc, ctx, "consts")
        ctx.enter_context(nc.Block())
        zero = made.did(pool.memset(ident[:], 0.0))
        made.wait(pool, zero)
        made.did(pool.affine_select(out=ident[:], in_=ident[:], compare_op=ALU.not_equal, fill=1.0, base=0,
                                    pattern=[[-1, P]], channel_multiplier=1))
        made.did(pool.memset(ones[:], 1.0))
    io = {**io, "ident": ident, "ones": ones}

    with ExitStack() as ctx:
        banks = [ctx.enter_context(nc.psum_tensor(f"bank{i}", [P, D], F32)) for i in range(8)]
        gram = [banks[0:4], banks[4:8]]
        context_and_gram(nc, io, mem, kv, col_sb, gram, fold_w)
        mem.at = kept_fold
        top = mem.end
        m_base = (top - 2 * B * KT * D * 4) // 32 * 32
        mem.at = m_base
        m_hi, m_lo = mem.pair("m", [P, B, KT, D])
        mem.at = m_base - KT * D * 4
        w_q_raw = mem.place("w_q_raw", [P, KT, D])
        mem.at, mem.end = kept_fold, m_base - KT * D * 4
        fold(nc, io, mem, kv, col_sb, gram, banks, fold_w, (m_hi, m_lo), c_row, w_q_raw)
    with ExitStack() as ctx:
        pairs = [ctx.enter_context(nc.psum_tensor(f"scores{i}", [P, 2, D], F32)) for i in range(2)]
        turned = ctx.enter_context(nc.psum_tensor("turned", [P, 2 * D], F32))
        value = ctx.enter_context(nc.psum_tensor("value", [P, D], F32))
        nxt = ctx.enter_context(nc.psum_tensor("next", [P, D], F32))
        mem.at, mem.end = kept_kv, m_base
        attend(nc, io, mem, kv, col_sb, {"scores": pairs, "turned": turned, "value": value, "next": nxt},
               (m_hi, m_lo), c_row, w_q_raw, (x1_dram, o_dram))
    with ExitStack() as ctx:
        banks = [ctx.enter_context(nc.psum_tensor(f"feed_bank{i}", [P, D], F32)) for i in range(8)]
        mem.at, mem.end = keep, top
        feed(nc, io, mem, col_sb, banks, (x1_dram, o_dram), out)


def kernel(**inputs):
    import concourse.bacc as bacc
    from concourse.bass_utils import run_bass_kernel_spmd

    a = {k: np.asarray(v) for k, v in inputs.items()}
    flat = np.ascontiguousarray
    heads = D // SELF_DH
    by_head = lambda w: w.reshape((3, SELF_DH, heads) + w.shape[1:]).swapaxes(1, 2).reshape((3, D) + w.shape[1:])
    w_q, w_k, w_v = by_head(a["L0_attn_w_qkv"])
    b_q, b_k, b_v = by_head(a["L0_attn_b_qkv"])
    cols = {"self_bq": b_q, "self_bv": b_v, "cross_bq": a["L0_xattn_b_q"], "cross_bk": a["L0_xattn_b_k"],
            "mu_r": a["L0_ffn_mu_r"], "mu_k": a["L0_ffn_mu_k"]}
    rows = {"self_bk": b_k, "self_bv_row": b_v, "self_bo": a["L0_attn_b_o"], "cross_bv": a["L0_xattn_b_v"],
            "cross_bo": a["L0_xattn_b_o"]}
    arrays = {
        "x_rows": flat(a["x"].reshape(B * S, D)),
        "x_cols": flat(a["x"].reshape(B * S, D).T),
        "ctx_cols": flat(a["ctx_1024"].reshape(B * CTX, D).T),
        "mask": flat(a["mask_Bx1xSxS2_ik1"].reshape(B * S, CTX)),
        "cols": flat(np.concatenate([cols[c].reshape(KT, P).T for c in COLS], axis=1)),
        "rows": flat(np.stack([rows[r] for r in ROWS])),
        "self_wq": flat(w_q), "self_wk": flat(w_k.T), "self_wv": flat(w_v.T), "self_wo": flat(a["L0_attn_w_o"].T),
        "cross_wq": flat(a["L0_xattn_W_q"].T), "cross_wk": flat(a["L0_xattn_W_k"].T),
        "cross_wv": flat(a["L0_xattn_W_v"].T), "cross_wo": flat(a["L0_xattn_W_o"].T),
        "ffn_wr": flat(a["L0_ffn_W_r"].T), "ffn_wk": flat(a["L0_ffn_W_k"].T), "ffn_wv": flat(a["L0_ffn_W_v"].T),
    }
    nc = bacc.Bacc("TRN2", target_bir_lowering=False, num_devices=1)
    io = {n: nc.dram_tensor(n, v.shape, mybir.dt.from_np(v.dtype), kind="ExternalInput").ap() for n, v in arrays.items()}
    out = nc.dram_tensor("out", (B * S, D), F32, kind="ExternalOutput").ap()
    decoder_layer(nc, io, out)
    r = run_bass_kernel_spmd(nc, [arrays], core_ids=[0])
    return r.results[0]["out"].reshape(B, S, D)
```

```python
import numpy as np
import concourse.bass as bass
from concourse import mybir
from concourse.alu_op_type import AluOpType as ALU

F32 = mybir.dt.float32
F32R = mybir.dt.float32r
I32 = mybir.dt.int32
ACT = mybir.ActivationFunctionType

P = 128
B, S, D = 2, 2048, 512
KT = D // P
CTX = 154
HEADS, DK = 16, D // 16
HPG = P // DK
HG = HEADS // HPG
GK = HPG * CTX
HALF = GK // 2
CH = -(-GK // P)
SELF_DH = 64
GT = 256
TPG = GT // P
NG = B * S // GT
UNITS = HG * TPG
EPS = 1e-5
SCALE = float(DK) ** -0.5
NEG = -float(2.0 ** 100)
HUGE = 3.0e38

COLS = ("self_bq", "self_bv", "cross_bq", "cross_bk", "mu_r", "mu_k")
FEED_WEIGHTS = ("cross_wo", "ffn_wk", "ffn_wr", "ffn_wv")
ROWS = ("self_bk", "self_bv_row", "self_bo", "cross_bv", "cross_bo")


class Signal:

    def __init__(self, nc, ctx, name, per, producer, step=1, done=0):
        self.sem = ctx.enter_context(nc.semaphore(name))
        self.per, self.step = per, step
        producer.sem_inc(self.sem, (1 + done) * per * step)

    def by(self, instruction):
        instruction.then_inc(self.sem, self.step)

    def wait(self, engine, n, k):
        engine.wait_ge(self.sem, (n * self.per + (self.per + k)) * self.step)


class Count:

    def __init__(self, nc, ctx, name, step=1):
        self.sem, self.n, self.step = ctx.enter_context(nc.semaphore(name)), 0, step

    def did(self, instruction):
        instruction.then_inc(self.sem, self.step)
        self.n += self.step
        return self.n

    def wait(self, engine, value=None):
        engine.wait_ge(self.sem, self.n if value is None else value)


class Map:

    def __init__(self, nc):
        self.nc, self.at, self.end = nc, -(-nc.sbuf_base // 32) * 32, nc.sbuf_usable_end

    def place(self, name, shape, dtype=F32):
        size = 4 * int(np.prod(shape[1:]))
        t = self.nc.alloc_sbuf_tensor_at(name, list(shape), dtype, offset=self.at)
        self.at += -(-size // 32) * 32
        assert self.at <= self.end, (name, self.at, self.end)
        return t

    def pair(self, name, shape):
        return self.place(name + "_hi", shape, F32R), self.place(name + "_lo", shape, F32R)

    def joined_pair(self, name, shape, axis):
        both = self.place(name, shape[:axis] + [2] + shape[axis:], F32R)
        half = lambda i: both[(slice(None),) * axis + (i,)]
        return both, half(0), half(1)


def f32(ap):
    return ap.bitcast(F32)


def three_pass(pe, out, sta, mov, first=True, last=True):
    pe.matmul(out, sta[0], mov[0], start=first, stop=False, skip_group_check=True)
    pe.matmul(out, sta[0], mov[1], start=False, stop=False, skip_group_check=True)
    return pe.matmul(out, sta[1], mov[0], start=False, stop=last, skip_group_check=True)


def context_and_gram(nc, io, mem, kv, col_sb, gram, fold_w, m_base):
    from contextlib import ExitStack

    x_sum, k_both, v_both = kv[4:]
    sp, act, pe, dve, pool = nc.sync, nc.scalar, nc.tensor, nc.vector, nc.gpsimd
    rows_of = [(r, min(P, B * CTX - r)) for r in range(0, B * CTX, P)]
    RING = 4
    with ExitStack() as ctx:
        ctx_t = mem.place("ctx_t", [P, KT, B * CTX])
        w_k = mem.place("w_k_raw", [P, KT, D])
        w_v = mem.place("w_v_raw", [P, KT, D])
        bv_row = mem.place("cross_bv_row", [P, D])
        v_raw = mem.place("v_raw", [P, len(rows_of), D])
        x_in = [mem.place(f"x_in{i}", [P, D]) for i in range(RING)]
        x_hi = [mem.place(f"x_hi{i}", [P, D], F32R) for i in range(RING)]
        x_lo = [mem.place(f"x_lo{i}", [P, D], F32R) for i in range(RING)]
        assert mem.at <= m_base
        mem.at = m_base
        kt, kt_hi, kt_lo = mem.joined_pair("kt", [P, KT, B * CTX], 1)
        vn, vn_hi, vn_lo = mem.joined_pair("vn", [P, len(rows_of), D], 2)

        block = ctx.enter_context(nc.Block())
        loads = [Count(nc, ctx, f"ctx_load{i}", 16) for i in range(5)]
        weights_in = Count(nc, ctx, "fold_weights_in", 16)
        mm = Count(nc, ctx, "ctx_mm")
        on_dve = Count(nc, ctx, "ctx_dve")
        on_act = Count(nc, ctx, "ctx_act")
        zeroed = Count(nc, ctx, "kv_zeroed")
        alone = ctx.enter_context(nc.semaphore("alone_gram"))

        def stands_alone(engine):
            engine.sem_inc(alone, 1)

        sum_zero = zeroed.did(pool.memset(x_sum[:], 0.0))
        for t in (v_both, k_both):
            zeroed.did(pool.memset(f32(t[:]), 0.0))

        PASSES = S // P // RING
        x_here = [Signal(nc, ctx, f"x_here{i}", 1, sp, 16) for i in range(RING)]
        split_hi = Signal(nc, ctx, "gram_hi", RING, act)
        split_lo = Signal(nc, ctx, "gram_lo", RING, dve)
        summed = Signal(nc, ctx, "gram_sum", RING, pool)
        used = Signal(nc, ctx, "gram_mm", RING, pe)

        def gram_load(n):
            for t in range(RING):
                split_lo.wait(sp, n - 1, t + 1)
                summed.wait(sp, n - 1, t + 1)
                stands_alone(sp)
                x_here[t].by(sp.dma_start(x_in[t][:], io["x_rows"][bass.ds((n * RING + t) * P, P), :]))

        def gram_pass(b, n, first, last):
            for t in range(RING):
                x_here[t].wait(act, n, 1)
                used.wait(act, n - 1, t + 1)
                split_hi.by(act.activation(x_hi[t][:], x_in[t][:], ACT.Copy))
                split_hi.wait(dve, n, t + 1)
                used.wait(dve, n - 1, t + 1)
                split_lo.by(dve.tensor_tensor(x_lo[t][:], x_in[t][:], f32(x_hi[t][:]), ALU.subtract))
                x_here[t].wait(pool, n, 1)
                summed.wait(pool, n, t)
                summed.by(pool.tensor_tensor(x_sum[:, b, :], x_sum[:, b, :], x_in[t][:], ALU.add))
                split_lo.wait(pe, n, t + 1)
                for i in range(KT):
                    c0 = min(i * P, D - 2 * P)
                    cols = slice(i * P, (i + 1) * P)
                    m = three_pass(pe, gram[b][i][:, c0:D], (x_hi[t][:, cols], x_lo[t][:, cols]),
                                   (x_hi[t][:, c0:D], x_lo[t][:, c0:D]),
                                   first=first and t == 0, last=last and t == RING - 1)
                used.by(m)

        gram_load(0)
        x_here[0].wait(act, 0, 1)
        loads[0].did(act.dma_start(ctx_t[:], io["ctx_cols"].rearrange("(k p) n -> p k n", p=P)))
        loads[1].did(act.dma_start(w_v[:], io["cross_wv"].rearrange("(k p) n -> p k n", p=P)))
        loads[2].did(act.dma_start(w_k[:], io["cross_wk"].rearrange("(k p) n -> p k n", p=P)))
        loads[3].did(act.dma_start(bv_row[:], io["rows"][3:4, :].broadcast_to([P, D])))
        loads[4].did(act.dma_start(col_sb[:], io["cols"]))
        zeroed.wait(pool, sum_zero)
        gram_pass(0, 0, True, False)

        loads[0].wait(pe)
        loads[1].wait(pe)
        v_ready = []
        for r, (r0, rn) in enumerate(rows_of):
            for k in range(KT):
                m = pe.matmul(gram[1][r][0:rn, :], ctx_t[:, k, r0:r0 + rn], w_v[:, k, :],
                              start=(k == 0), stop=(k == KT - 1))
            v_ready.append(mm.did(m))
        loads[3].wait(dve)
        v_read = []
        for r, (r0, rn) in enumerate(rows_of):
            mm.wait(dve, v_ready[r])
            v_read.append(on_dve.did(dve.tensor_tensor(v_raw[0:rn, r, :], gram[1][r][0:rn, :], bv_row[0:rn, :],
                                                       ALU.add)))
            on_dve.wait(act, v_read[r])
            hi = on_act.did(act.activation(vn_hi[0:rn, r, :], v_raw[0:rn, r, :], ACT.Copy))
            on_act.wait(dve, hi)
            v_done = on_dve.did(dve.tensor_tensor(vn_lo[0:rn, r, :], v_raw[0:rn, r, :],
                                                  f32(vn_hi[0:rn, r, :]), ALU.subtract))
        loads[2].wait(pe)
        loads[4].wait(act)
        loads[4].wait(dve)
        bk = col_sb[:, 3 * KT:4 * KT]
        for m4 in range(KT):
            bank = gram[1][(m4 - 1) % KT]
            if m4:
                on_dve.wait(pe, v_read[m4 - 1])
            for k in range(KT):
                m = pe.matmul(bank[:, 0:B * CTX], w_k[:, k, m4 * P:(m4 + 1) * P], ctx_t[:, k, :],
                              start=(k == 0), stop=(k == KT - 1))
            done = mm.did(m)
            mm.wait(act, done)
            hi = on_act.did(act.activation(kt_hi[:, m4, :], bank[:, 0:B * CTX], ACT.Identity,
                                           bias=bk[:, m4:m4 + 1]))
            on_act.wait(dve, hi)
            k_done = on_dve.did(dve.scalar_tensor_tensor(kt_lo[:, m4, :], bank[:, 0:B * CTX],
                                                         bk[:, m4:m4 + 1], f32(kt_hi[:, m4, :]),
                                                         ALU.add, ALU.subtract))

        with nc.Fori(1, PASSES - 1) as n:
            gram_load(n)
            gram_pass(0, n, False, False)
        gram_load(PASSES - 1)
        gram_pass(0, PASSES - 1, False, True)
        gram_load(PASSES)
        on_dve.wait(pe, k_done)
        gram_pass(1, PASSES, True, False)
        weights_in.did(act.dma_start(fold_w["self_wv"][:], io["self_wv"].rearrange("(k p) n -> p k n", p=P)))
        with nc.Fori(PASSES + 1, 2 * PASSES - 1) as n:
            gram_load(n)
            gram_pass(1, n, False, False)
        gram_load(2 * PASSES - 1)
        gram_pass(1, 2 * PASSES - 1, False, True)
        weights_in.wait(sp)
    placements = []
    for j in range(HPG):
        for b in range(B):
            key = 0
            while key < CTX:
                row, flat = b * CTX + key, j * CTX + key
                n = min(CTX - key, P - row % P, P - flat % P)
                placements.append((
                    v_both[flat % P:flat % P + n, b, flat // P]
                    .rearrange("p x g f -> p (x g) f")[:, :, j * DK:(j + 1) * DK],
                    vn[row % P:row % P + n, row // P]
                    .rearrange("p x (g f) -> p (x g) f", g=HG)[:, :, j * DK:(j + 1) * DK]))
                key += n
            for row in (j % 2 * DK, (j % 2 + 2) * DK):
                placements.append((
                    k_both[row:row + DK, b].rearrange("p x g n -> p (x g) n")[:, :, j * CTX:(j + 1) * CTX],
                    kt[j * DK:(j + 1) * DK].rearrange("p x k n -> p (x k) n")[:, :, b * CTX:(b + 1) * CTX]))
    return placements


def fold(nc, io, mem, kv, col_sb, gram, psum8, fold_w, m_out, c_row, w_q_raw, placements, early):
    from contextlib import ExitStack

    x_sum = kv[4]
    m_hi, m_lo = m_out
    wq_hi, wq_lo, x_in, xt_hi, xt_lo = early
    ident, ones = io["ident"], io["ones"]
    sp, act, pe, dve, pool = nc.sync, nc.scalar, nc.tensor, nc.vector, nc.gpsimd
    with ExitStack() as ctx:
        g = mem.place("g_then_u", [P, B, KT, D])
        t = mem.place("t_then_m", [P, B, KT, D])
        kv_t = mem.place("kv_t", [P, B, KT, P])
        rows = mem.place("self_rows", [P, 3, D])
        s_col = mem.place("s_col", [P, B, KT])
        t0_col = mem.place("t0_col", [P, B, KT])
        bq_wide = mem.place("bq_wide", [P, KT, P])

        ctx.enter_context(nc.Block())
        rows_in = Count(nc, ctx, "self_rows_in", 16)
        wq_in = Count(nc, ctx, "cross_wq_in", 16)
        x_here = Count(nc, ctx, "first_x_in", 16)
        placed = Count(nc, ctx, "kv_placed", 16)
        weights_in = {name: Count(nc, ctx, name + "_in", 16) for name in ("self_wk", "self_wo", "self_wq")}
        mm = Count(nc, ctx, "fold_mm")
        dv = Count(nc, ctx, "fold_dve")
        ac = Count(nc, ctx, "fold_act")
        pz = Count(nc, ctx, "fold_pool")

        for name, c in weights_in.items():
            c.did(sp.dma_start(fold_w[name][:], io[name].rearrange("(k p) n -> p k n", p=P)))
        for r in range(3):
            rows_in.did(sp.dma_start(rows[:, r, :], io["rows"][r:r + 1, :].broadcast_to([P, D])))
        wq_in.did(sp.dma_start(w_q_raw[:], io["cross_wq"].rearrange("(k p) n -> p k n", p=P)))
        for dst, src in placements:
            placed.did(sp.dma_start(f32(dst), f32(src)))
        pz.did(pool.memset(kv_t[:], 0.0))

        g_done = []
        for b in range(B):
            for i in range(KT):
                c0 = min(i * P, D - 2 * P)
                if i % 2:
                    g_done.append((ac, ac.did(act.activation(g[:, b, i, c0:D], gram[b][i][:, c0:D], ACT.Copy))))
                else:
                    g_done.append((dv, dv.did(dve.tensor_copy(g[:, b, i, c0:D], gram[b][i][:, c0:D]))))
        for k in range(KT):
            bq = dv.did(dve.tensor_scalar(bq_wide[:, k, :], ones[:], col_sb[:, k:k + 1], None, ALU.mult))
        lower = [(i, j) for i in range(KT) for j in range(i) if j * P < min(i * P, D - 2 * P)]
        for c, v in g_done:
            c.wait(pe, v)
        small = {}
        for b in range(B):
            for k in range(KT):
                m = pe.matmul(psum8[2 * b][:, k:k + 1], x_sum[:, b, k * P:(k + 1) * P], ones[:, 0:1],
                              start=True, stop=True)
            small[b] = mm.did(m)
        mirrored = {}
        for b in range(B):
            for n, (i, j) in enumerate(lower):
                bank = psum8[2 * b + 1] if n < KT else psum8[4 + b]
                m = pe.transpose(bank[:, (n % KT) * P:(n % KT + 1) * P], g[:, b, j, i * P:(i + 1) * P], ident[:])
            mirrored[b] = mm.did(m)
        g_whole, s_done = {}, {}
        for b in range(B):
            mm.wait(dve, small[b])
            s_done[b] = dv.did(dve.tensor_copy(s_col[:, b, :], psum8[2 * b][:, 0:KT]))
            mm.wait(dve, mirrored[b])
            for n, (i, j) in enumerate(lower):
                bank = psum8[2 * b + 1] if n < KT else psum8[4 + b]
                g_whole[b] = dv.did(dve.tensor_copy(g[:, b, i, j * P:(j + 1) * P],
                                                    bank[:, (n % KT) * P:(n % KT + 1) * P]))

        w_v, w_k, w_o, w_q = (fold_w[n] for n in ("self_wv", "self_wk", "self_wo", "self_wq"))
        rows_in.wait(dve)
        t_done = {}
        last_read = {}
        order = [6, 7, 4, 5, 0, 1, 2, 3]
        turn = [0]

        def next_bank():
            n = order[turn[0] % 8]
            turn[0] += 1
            if n in last_read:
                c, v = last_read[n]
                c.wait(pe, v)
            return n, psum8[n]

        for b in range(B):
            last_read[2 * b] = (dv, s_done[b])
            last_read[2 * b + 1] = last_read[4 + b] = (dv, g_whole[b])
        for b in range(B):
            dv.wait(pe, g_whole[b])
            for i in range(KT):
                n, bank = next_bank()
                for k in range(KT):
                    m = pe.matmul(bank[:], g[:, b, k, i * P:(i + 1) * P], w_v[:, k, :],
                                  start=(k == 0), stop=(k == KT - 1))
                v = mm.did(m)
                mm.wait(dve, v)
                dv.wait(dve, s_done[b])
                t_done[b] = dv.did(dve.scalar_tensor_tensor(t[:, b, i, :], rows[:, 1, :], s_col[:, b, i:i + 1],
                                                            bank[:], ALU.mult, ALU.add))
                last_read[n] = (dv, t_done[b])
        t0_done = {}
        n, bank = next_bank()
        by_batch = bank[:, 0:KT * B].rearrange("p (q b) -> p q b", b=B)
        for q in range(KT):
            for k in range(KT):
                m = pe.matmul(by_batch[:, q, :], w_v[:, k, q * P:(q + 1) * P], s_col[:, :, k],
                              start=(k == 0), stop=(k == KT - 1))
        v = mm.did(m)
        mm.wait(dve, v)
        for b in range(B):
            t0_done[b] = dv.did(dve.scalar_tensor_tensor(t0_col[:, b, :], col_sb[:, KT:2 * KT], float(S),
                                                         by_batch[:, :, b], ALU.mult, ALU.add))
        last_read[n] = (dv, t0_done[B - 1])
        pz.wait(dve)
        kv_done, u_done = {}, {}
        weights_in["self_wk"].wait(pe)
        for b in range(B):
            dv.wait(pe, t_done[b])
            n, bank = next_bank()
            for q in range(KT):
                for k in range(KT):
                    m = pe.matmul(bank[:, q * P:(q + 1) * P], t[:, b, k, q * P:(q + 1) * P],
                                  w_k[:, k, q * P:(q + 1) * P], start=(k == 0), stop=(k == KT - 1))
            v = mm.did(m)
            mm.wait(dve, v)
            dv.wait(dve, t0_done[b])
            for q in range(KT):
                for h in range(2):
                    r = slice(h * SELF_DH, (h + 1) * SELF_DH)
                    c = slice(q * P + h * SELF_DH, q * P + (h + 1) * SELF_DH)
                    kv_done[b] = dv.did(dve.scalar_tensor_tensor(
                        kv_t[r, b, q, r], rows[r, 0, c], t0_col[r, b, q:q + 1], bank[r, c], ALU.mult, ALU.add))
            last_read[n] = (dv, kv_done[b])
        wq_in.wait(act)
        wq_in.wait(dve)
        mm.wait(act)
        mm.wait(dve)
        wq_high = ac.did(act.activation(wq_hi[:], w_q_raw[:], ACT.Copy))
        ac.wait(dve, wq_high)
        dv.did(dve.tensor_tensor(wq_lo[:], w_q_raw[:], f32(wq_hi[:]), ALU.subtract))
        for b in range(B):
            mm.wait(sp, small[b])
        x_here.did(sp.dma_start(x_in[:], io["x_cols"].rearrange("(k p) n -> p k n", p=P)[:, :, 0:GT]))
        weights_in["self_wo"].wait(pe)
        for b in range(B):
            dv.wait(pe, kv_done[b])
            for q in range(KT):
                n, bank = next_bank()
                v = mm.did(pe.matmul(bank[:], kv_t[:, b, q, :], w_o[:, q, :], start=True, stop=True))
                mm.wait(act, v)
                u_done[b] = ac.did(act.activation(g[:, b, q, :], bank[:], ACT.Copy))
                last_read[n] = (ac, u_done[b])
        x_here.wait(act)
        x_here.wait(dve)
        mm.wait(act)
        mm.wait(dve)
        x_high = ac.did(act.activation(xt_hi[:], x_in[:], ACT.Copy))
        ac.wait(dve, x_high)
        dv.did(dve.tensor_tensor(xt_lo[:], x_in[:], f32(xt_hi[:]), ALU.subtract))
        for b in range(B):
            ac.wait(pe, u_done[b])
            dv.wait(pe, bq)
            n, bank = next_bank()
            for q in range(KT):
                m = pe.matmul(bank[:], bq_wide[:, q, :], g[:, b, q, :], start=(q == 0), stop=(q == KT - 1))
            v = mm.did(m)
            mm.wait(dve, v)
            last_read[n] = (dv, dv.did(dve.tensor_tensor(c_row[:, b, :], bank[:], rows[:, 2, :], ALU.add)))
        placed.wait(act)
        placed.wait(dve)
        weights_in["self_wq"].wait(pe)
        for b in range(B):
            for i in range(KT):
                n, bank = next_bank()
                for q in range(KT):
                    m = pe.matmul(bank[:], w_q[:, q, i * P:(i + 1) * P], g[:, b, q, :],
                                  start=(q == 0), stop=(q == KT - 1))
                v = mm.did(m)
                mm.wait(act, v)
                copied = ac.did(act.activation(t[:, b, i, :], bank[:], ACT.Copy))
                last_read[n] = (ac, copied)
                ac.wait(dve, copied)
                eye = dv.did(dve.tensor_tensor(t[:, b, i, i * P:(i + 1) * P], t[:, b, i, i * P:(i + 1) * P],
                                               ident[:], ALU.add))
                dv.wait(act, eye)
                hi = ac.did(act.activation(m_hi[:, b, i, :], t[:, b, i, :], ACT.Copy))
                ac.wait(dve, hi)
                dv.did(dve.tensor_tensor(m_lo[:, b, i, :], t[:, b, i, :], f32(m_hi[:, b, i, :]), ALU.subtract))


def attend(nc, io, mem, kv, col_sb, psum, m_in, c_row, early, scratch, feed_raw, feed_raw_in, feed_first,
           o_kept):
    from contextlib import ExitStack

    k_hi, k_lo, v_hi, v_lo = kv[:4]
    m_hi, m_lo = m_in
    ident = io["ident"]
    x1_dram, o_dram = scratch
    sp, act, pe, dve, pool = nc.sync, nc.scalar, nc.tensor, nc.vector, nc.gpsimd
    BUFS = 4
    LEAD = 3
    with ExitStack() as ctx:
        wq_hi, wq_lo, x_in, xt_hi, xt_lo = early
        x1 = mem.place("x1", [P, TPG, D])
        x1t_hi, x1t_lo = mem.pair("x1t", [P, KT, GT])
        q = mem.place("q", [P, HG, 2, GT], F32R)
        prob = [mem.place(f"prob{i}", [P, CH * P]) for i in range(BUFS)]
        at, mem.at = mem.at, mem.end - HG * GT * 4
        out_t = mem.place("out_t", [P, HG, GT])
        mem.at, mem.end = at, mem.end - HG * GT * 4
        mask_in = mem.place("mask_in", [P, TPG, CTX], I32)
        mask_add = [mem.place(f"mask_add{i}", [P, TPG, CTX]) for i in range(B)]
        stats = mem.place("stats", [P, TPG, 6])
        moments = mem.place("moments", [P, TPG, 2])
        var_eps = mem.place("var_eps", [P, TPG])
        rstd = mem.place("rstd", [P, TPG])
        neg_half = mem.place("neg_half", [P, TPG])
        minus_one = mem.place("minus_one", [P, HPG])
        row_min = mem.place("row_min", [P, BUFS, HPG])
        row_sum = mem.place("row_sum", [P, BUFS, HPG])
        row_inv = mem.place("row_inv", [P, BUFS, HPG])
        pt = [mem.pair(f"prob_t{i}", [P, CH, GT]) for i in range(2)]

        ctx.enter_context(nc.Block())
        setup = Count(nc, ctx, "attend_constants")
        first_o, first_x1 = Count(nc, ctx, "first_o_in", 16), Count(nc, ctx, "first_x1_in", 16)
        first_bo = Count(nc, ctx, "first_bo_in", 16)
        first_hi, first_lo, first_pool = (Count(nc, ctx, "first_" + x) for x in ("hi", "wo_lo", "pool"))
        alone = ctx.enter_context(nc.semaphore("alone_attend"))
        sig = lambda name, per, eng, step=1, done=0: Signal(nc, ctx, name, per, eng, step, done)
        x_here = sig("x_here", 1, sp, 16, 1)
        x_hi_ok, x_lo_ok = sig("x_hi_ok", 1, act, 1, 1), sig("x_lo_ok", 1, pool, 1, 1)
        y_mm, y_read = sig("y_mm", TPG, pe), sig("y_read", TPG, dve)
        y_stat, y_mom = sig("y_stat", TPG, dve), sig("y_mom", TPG, dve)
        y_var, y_rstd = sig("y_var", 1, dve), sig("y_rstd", 1, pool)
        x1_ok, x1_kept = sig("x1_ok", TPG, dve), sig("x1_kept", 1, sp, 16)
        tr_mm, x1t_hi_ok, x1t_lo_ok = sig("tr_mm", TPG, pe), sig("x1t_hi_ok", TPG, act), sig("x1t_lo_ok", TPG, dve)
        q_mm, q_hi_ok, q_lo_ok = sig("q_mm", 2, pe), sig("q_hi_ok", 2, act), sig("q_lo_ok", 2, dve)
        mask_here, mask_ok = sig("mask_here", 1, sp, 16), sig("mask_ok", 1, dve)
        s_mm, s_min = sig("s_mm", UNITS, pe), sig("s_min", UNITS, dve)
        p_exp, p_inv, p_norm = sig("p_exp", UNITS, act), sig("p_inv", UNITS, pool), sig("p_norm", UNITS, pool)
        t_mm, t_hi_ok, t_lo_ok = sig("t_mm", UNITS, pe), sig("t_hi_ok", UNITS, act), sig("t_lo_ok", UNITS, dve)
        pv_mm, o_read = sig("pv_mm", HG, pe), sig("o_read", HG, act)

        def stands_alone(engine):
            engine.sem_inc(alone, 1)

        def token0(b, j):
            return j * GT + b * S

        for t in prob:
            setup.did(pool.memset(t[:, GK:CH * P], 0.0))
        setup.did(pool.memset(minus_one[:], -1.0))
        pad_ok = setup.did(pool.memset(neg_half[:], -0.5))
        setup.wait(dve, pad_ok)
        setup.wait(pool, pad_ok)

        def load_x(n, b, j):
            x_hi_ok.wait(sp, n - 1, 1)
            x_lo_ok.wait(sp, n - 1, 1)
            stands_alone(sp)
            x_here.by(sp.dma_start(x_in[:], io["x_cols"].rearrange("(k p) n -> p k n", p=P)
                                   [:, :, bass.ds(token0(b, j), GT)]))

        def load_mask(n, b, j):
            mask_ok.wait(sp, n - 1, 1)
            stands_alone(sp)
            mask_here.by(sp.dma_start(mask_in[:], io["mask"][bass.ds(token0(b, j), GT), :]
                                      .rearrange("(t p) c -> p t c", p=P)))

        def split_x(n):
            x_here.wait(act, n, 1)
            y_mm.wait(act, n - 1, TPG)
            x_hi_ok.by(act.activation(xt_hi[:], x_in[:], ACT.Copy))
            x_hi_ok.wait(pool, n, 1)
            y_mm.wait(pool, n - 1, TPG)
            x_lo_ok.by(pool.tensor_tensor(xt_lo[:], x_in[:], f32(xt_hi[:]), ALU.subtract))

        def make_mask(n, b):
            mask_here.wait(dve, n, 1)
            if not (isinstance(n, int) and n == 0):
                s_min.wait(dve, n - B, UNITS)
            mask_ok.by(dve.tensor_scalar(mask_add[b][:], mask_in[:], 0.0, NEG, ALU.is_equal, ALU.mult))

        def y_product(n, b, t, bank="next"):
            if t == 0:
                q_lo_ok.wait(pe, n - 1, 2)
                x_hi_ok.wait(pe, n, 1)
                x_lo_ok.wait(pe, n, 1)
            elif bank == "next":
                y_read.wait(pe, n, t)
            for k in range(KT):
                cols = slice(t * P, (t + 1) * P)
                m = three_pass(pe, psum[bank][:], (xt_hi[:, k, cols], xt_lo[:, k, cols]),
                               (m_hi[:, b, k, :], m_lo[:, b, k, :]), first=(k == 0), last=(k == KT - 1))
            y_mm.by(m)

        def y_finish(n, b, t, bank="next"):
            y_mm.wait(dve, n, t + 1)
            if t == 0:
                tr_mm.wait(dve, n - 1, TPG)
                x1_kept.wait(dve, n - 1, 1)
            y_read.by(dve.tensor_tensor(x1[:, t, :], psum[bank][:], c_row[:, b, :], ALU.add))
            y_read.wait(dve, n, t + 1)
            y_stat.by(dve.bn_stats(stats[:, t, :], x1[:, t, :]))
            y_stat.wait(dve, n, t + 1)
            stands_alone(dve)
            y_mom.by(dve.bn_aggr(moments[:, t, :], stats[:, t, :]))
            if t == TPG - 1:
                y_mom.wait(dve, n, TPG)
                y_rstd.wait(dve, n - 1, 1)
                y_var.by(dve.tensor_scalar(var_eps[:], moments[:, :, 1], EPS, None, ALU.add))
                y_var.wait(pool, n, 1)
                x1_ok.wait(pool, n - 1, TPG)
                y_rstd.by(pool.tensor_tensor(rstd[:], var_eps[:], neg_half[:], ALU.pow))

        def x1_finish(n, b, j):
            y_rstd.wait(dve, n, 1)
            for t in range(TPG):
                x1_ok.by(dve.tensor_scalar(x1[:, t, :], x1[:, t, :], moments[:, t, 0:1], rstd[:, t:t + 1],
                                           ALU.subtract, ALU.mult))
            x1_ok.wait(sp, n, TPG)
            stands_alone(sp)
            x1_kept.by(sp.dma_start(x1_dram[bass.ds(token0(b, j), GT), :].rearrange("(t p) d -> p t d", p=P), x1[:]))

        def x1_transpose(n, t):
            bank = psum["next"] if t == 0 else psum["value"]
            x1_ok.wait(pe, n, t + 1)
            if t == 0:
                y_read.wait(pe, n, TPG)
            else:
                o_read.wait(pe, n - 1, 1)
            for k in range(KT):
                m = pe.transpose(bank[:, k * P:(k + 1) * P], x1[:, t, k * P:(k + 1) * P], ident[:])
            tr_mm.by(m)

        def x1t_split(n, t):
            bank = (psum["next"] if t == 0 else psum["value"])[:].rearrange("p (k n) -> p k n", k=KT)
            cols = slice(t * P, (t + 1) * P)
            tr_mm.wait(act, n, t + 1)
            q_mm.wait(act, n - 1, 2)
            x1t_hi_ok.by(act.activation(x1t_hi[:, :, cols], bank, ACT.Copy))
            x1t_hi_ok.wait(dve, n, t + 1)
            x1t_lo_ok.by(dve.tensor_tensor(x1t_lo[:, :, cols], bank, f32(x1t_hi[:, :, cols]), ALU.subtract))

        def q_product(n, h, bank="next"):
            if h == 0:
                x1t_lo_ok.wait(pe, n, TPG)
            elif bank == "next":
                q_lo_ok.wait(pe, n, h)
            for i in range(2):
                cols = slice((2 * h + i) * P, (2 * h + i + 1) * P)
                for k in range(KT):
                    m = three_pass(pe, psum[bank][:, i * GT:(i + 1) * GT], (wq_hi[:, k, cols], wq_lo[:, k, cols]),
                                   (x1t_hi[:, k, :], x1t_lo[:, k, :]), first=(k == 0), last=(k == KT - 1))
            q_mm.by(m)

        def q_split(n, h, bank="next"):
            q_mm.wait(act, n, h + 1)
            s_mm.wait(act, n - 1, UNITS * (h + 1) // 2)
            bq = col_sb[:, 2 * KT:3 * KT]
            piece = [(2 * h + i, pair, slice(pair * P // 2, (pair + 1) * P // 2),
                      slice(i * GT, (i + 1) * GT)) for i in range(2) for pair in range(2)]
            for g, pair, rows, cols in piece:
                m = act.activation(q[rows, g, pair, :], psum[bank][rows, cols], ACT.Identity, bias=bq[rows, g:g + 1])
            q_hi_ok.by(m)
            q_hi_ok.wait(dve, n, h + 1)
            for g, pair, rows, cols in piece:
                other = slice((1 - pair) * P // 2, (2 - pair) * P // 2)
                m = dve.scalar_tensor_tensor(q[other, g, pair, :], psum[bank][rows, cols], bq[rows, g:g + 1],
                                             f32(q[rows, g, pair, :]), ALU.add, ALU.subtract)
            q_lo_ok.by(m)

        def scores(n, b, u):
            g, t = divmod(u, TPG)
            bank = psum["scores"]
            if u % (UNITS // 2) == 0:
                q_lo_ok.wait(pe, n, 1 + u // (UNITS // 2))
            s_min.wait(pe, n, u)
            cols = slice(t * P, (t + 1) * P)
            for keys in (k_hi, k_lo):
                for h in range(2):
                    m = pe.matmul(bank[:, h, 0:HALF], q[:, g, h, cols], keys[:, b, g, h * HALF:(h + 1) * HALF],
                                  start=keys is k_hi, stop=keys is k_lo, skip_group_check=True)
            s_mm.by(m)

        def masked_min(n, b, u):
            t, buf = u % TPG, u % BUFS
            if u == 0:
                mask_ok.wait(dve, n, 1)
            s_mm.wait(dve, n, u + 1)
            t_mm.wait(dve, n, u + 1 - BUFS)
            stands_alone(dve)
            for h in range(HPG):
                m = dve.tensor_tensor_reduce(prob[buf][:, h * CTX:(h + 1) * CTX],
                                             psum["scores"][:, h // 2, (h % 2) * CTX:(h % 2 + 1) * CTX],
                                             mask_add[b][:, t, :], -SCALE, HUGE, ALU.add, ALU.min,
                                             row_min[:, buf, h:h + 1])
            s_min.by(m)

        def exponentials(n, u):
            buf = u % BUFS
            s_min.wait(act, n, u + 1)
            for h in range(HPG):
                keys = prob[buf][:, h * CTX:(h + 1) * CTX]
                m = act.activation(keys, keys, ACT.Exp, bias=row_min[:, buf, h:h + 1], scale=-1.0,
                                   accum_out=row_sum[:, buf, h:h + 1])
            p_exp.by(m)

        def normalise(n, u):
            buf = u % BUFS
            p_exp.wait(pool, n, u + 1)
            p_inv.by(pool.tensor_tensor(row_inv[:, buf, :], row_sum[:, buf, :], minus_one[:], ALU.pow))
            keys = prob[buf][:, 0:GK].rearrange("p (h c) -> p h c", h=HPG)
            p_inv.wait(pool, n, u + 1)
            p_norm.by(pool.tensor_tensor(keys, keys, row_inv[:, buf, :].unsqueeze(2).broadcast_to([P, HPG, CTX]),
                                         ALU.mult))

        def transposes(n, u):
            p_norm.wait(pe, n, u + 1)
            t_lo_ok.wait(pe, n, u - 1)
            for c in range(CH):
                m = pe.transpose(psum["turned"][u % 2][:, c * P:(c + 1) * P], prob[u % BUFS][:, c * P:(c + 1) * P], ident[:])
            t_mm.by(m)

        def transposed_split(n, u):
            g, t = divmod(u, TPG)
            hi, lo = (x[:, :, t * P:(t + 1) * P] for x in pt[g % 2])
            src = psum["turned"][u % 2][:, 0:CH * P].rearrange("p (c n) -> p c n", c=CH)
            t_mm.wait(act, n, u + 1)
            pv_mm.wait(act, n, g - 1)
            t_hi_ok.by(act.activation(hi, src, ACT.Copy))
            t_hi_ok.wait(dve, n, u + 1)
            t_lo_ok.by(dve.tensor_tensor(lo, src, f32(hi), ALU.subtract))

        def values(n, b, g, next_group):
            t_lo_ok.wait(pe, n, (g + 1) * TPG)
            o_read.wait(pe, n, g)
            if g == 1 and next_group:
                x1t_lo_ok.wait(pe, n + 1, TPG)
            hi, lo = pt[g % 2]
            for c in range(CH):
                m = three_pass(pe, psum["value"][:, 0:GT], (v_hi[:, b, c, g, :], v_lo[:, b, c, g, :]),
                               (hi[:, c, :], lo[:, c, :]), first=(c == 0), last=(c == CH - 1))
            pv_mm.by(m)
            pv_mm.wait(act, n, g + 1)
            if g == 0:
                o_kept.wait(act, n - 1, 1)
            o_read.by(act.activation(out_t[:, g, :], psum["value"][:, 0:GT], ACT.Copy))

        def store_values(n, b, j):
            o_read.wait(sp, n, HG)
            stands_alone(sp)
            o_kept.by(sp.dma_start(o_dram.rearrange("(g p) n -> p g n", p=P)[:, :, bass.ds(token0(b, j), GT)], out_t[:]))

        def unit(n, b, u, ahead):
            if u < UNITS:
                return n, b, u
            return (n + 1, (b + 1) % B, u - UNITS) if ahead else None

        def step(n, b, j, u, ahead, ahead2):
            b1, j1 = (b + 1) % B, j + (b + 1) // B
            if ahead and u == 1:
                y_finish(n + 1, b1, 0)
            transposes(n, u)
            if ahead and u == 2:
                y_finish(n + 1, b1, 1)
            if ahead2 and u == 6:
                split_x(n + 2)
            if ahead and u == 7:
                q_product(n + 1, 1)
            transposed_split(n, u)
            if ahead and u == 4:
                make_mask(n + 1, b1)
            if u == 6:
                values(n, b, 2, ahead)
            if (x := unit(n, b, u + LEAD, ahead)) is not None:
                scores(*x)
                masked_min(*x)
            if ahead and u == 7:
                q_split(n + 1, 1)
            if (x := unit(n, b, u + LEAD - 1, ahead)) is not None:
                exponentials(x[0], x[2])
                normalise(x[0], x[2])
            if ahead:
                if u < TPG:
                    y_product(n + 1, b1, u)
                if u == 2:
                    x1_finish(n + 1, b1, j1)
                if u == 3:
                    for t in range(TPG):
                        x1_transpose(n + 1, t)
                    for t in range(TPG):
                        x1t_split(n + 1, t)
                if u == 4:
                    q_product(n + 1, 0)
                    q_split(n + 1, 0)
            if u in (2, 4, 7):
                values(n, b, (2, 4, 6, 7).index(u), ahead)
            if u == UNITS - 1:
                store_values(n, b, j)

        def group(n, b, j, ahead, ahead2, near_end=lambda: None):
            b1, j1 = (b + 1) % B, j + (b + 1) // B
            if ahead:
                load_mask(n + 1, b1, j1)
            if ahead2:
                load_x(n + 2, b, j + 1)
            for u in range(UNITS):
                if u == UNITS - 2:
                    near_end()
                step(n, b, j, u, ahead, ahead2)

        load_mask(0, 0, 0)
        load_x(1, 1, 0)
        make_mask(0, 0)
        for t, bank in enumerate(("next", "value")):
            y_product(0, 0, t, bank)
            y_finish(0, 0, t, bank)
        split_x(1)
        x1_finish(0, 0, 0)
        for t in range(TPG):
            x1_transpose(0, t)
            x1t_split(0, t)
        q_product(0, 0)
        q_split(0, 0)
        q_product(0, 1, "value")
        for u in range(LEAD):
            if u == LEAD - 1:
                q_split(0, 1, "value")
            scores(0, 0, u)
            masked_min(0, 0, u)
            if u < LEAD - 1:
                exponentials(0, u)
                normalise(0, u)
        with nc.Fori(0, NG // B - 1) as j:
            for b in range(B):
                group(B * j + b, b, j, True, True)
        last = NG // B - 1
        group(B * last, 0, last, True, False)
        wo_hi, wo_lo, o_in, ot_hi, ot_lo, x1_in, bo_row = feed_first
        load_raw = lambda name: feed_raw_in[name].did(sp.dma_start(
            feed_raw[name][:], io[name].rearrange("(k p) n -> p k n", p=P)))
        y_mm.wait(sp, NG - 1, TPG)
        load_raw("cross_wo")
        o_kept.wait(sp, 0, 1)
        x_lo_ok.wait(sp, NG - 1, 1)
        first_o.did(sp.dma_start(o_in[:], o_dram.rearrange("(g p) n -> p g n", p=P)[:, :, 0:GT]))
        x1_kept.wait(sp, NG - 1, 1)
        tr_mm.wait(sp, NG - 1, TPG)
        first_x1.did(sp.dma_start(x1_in[:], x1_dram[0:GT, :].rearrange("(t p) d -> p t d", p=P)))
        y_read.wait(sp, NG - 1, TPG)
        first_bo.did(sp.dma_start(bo_row[:], io["rows"][4:5, :].broadcast_to([P, D])))
        for name in FEED_WEIGHTS[1:]:
            load_raw(name)

        def split_first():
            for eng in (act, dve):
                feed_raw_in["cross_wo"].wait(eng)
                q_mm.wait(eng, NG - 1, 2)
            wo_high = first_hi.did(act.activation(wo_hi[:], feed_raw["cross_wo"][:], ACT.Copy))
            first_hi.wait(dve, wo_high)
            first_lo.did(dve.tensor_tensor(wo_lo[:], feed_raw["cross_wo"][:], f32(wo_hi[:]), ALU.subtract))
            for eng in (act, pool):
                first_o.wait(eng)
                y_mm.wait(eng, NG - 1, TPG)
            ot_high = first_hi.did(act.activation(ot_hi[:], o_in[:], ACT.Copy))
            first_hi.wait(pool, ot_high)
            first_pool.did(pool.tensor_tensor(ot_lo[:], o_in[:], f32(ot_hi[:]), ALU.subtract))
            first_x1.wait(pool)
            first_bo.wait(pool)
            first_pool.did(pool.tensor_tensor(x1_in[:], x1_in[:], bo_row[:].unsqueeze(1).broadcast_to([P, TPG, D]),
                                              ALU.add))

        group(NG - 1, 1, last, False, False, split_first)
        x1_kept.wait(sp, NG - 1, 1)


def feed(nc, io, mem, col_sb, psum8, scratch, raw, raw_in, first, around_first, o_kept, out):
    from contextlib import ExitStack

    ident = io["ident"]
    x1_dram, o_dram = scratch
    sp, act, pe, dve, pool = nc.sync, nc.scalar, nc.tensor, nc.vector, nc.gpsimd
    o_bank, tr_bank, k_bank, rv_bank = psum8[0:2], psum8[2:4], psum8[4:6], psum8[6:8]
    with ExitStack() as ctx:
        wo_hi, wo_lo, o_in, ot_hi, ot_lo, x1_in, bo_row = first
        ot = (ot_hi, ot_lo)
        w = {"cross_wo": (wo_hi, wo_lo)} | {x: mem.pair(x, [P, KT, D]) for x in FEED_WEIGHTS[1:]}
        x2 = [mem.place(f"x2_{b}", [P, TPG, D]) for b in range(B)]
        x2t = [mem.place(f"x2_t{b}", [P, KT, 1 + GT]) for b in range(B)]
        diff = mem.place("diff", [P, KT, GT])
        mixed = {g: mem.place("mixed_" + g, [P, KT, GT]) for g in "kr"}
        assert mem.at <= around_first[0]
        mem.at = around_first[1]
        mix = {g: mem.pair("mix_" + g, [P, KT, GT]) for g in "kr"}
        relu = mem.place("relu", [P, KT, GT])
        square = mem.place("square", [P, KT, GT])
        ka = mem.pair("k_act", [P, KT, GT])
        gate = mem.place("gate", [P, TPG, D])
        y3 = mem.place("y3", [P, TPG, D])
        neg_half = mem.place("neg_half4", [P, TPG])
        norm = {k: (mem.place(f"stats_{k}", [P, TPG, 6]), mem.place(f"moments_{k}", [P, TPG, 2]),
                    mem.place(f"var_{k}", [P, TPG]), mem.place(f"rstd_{k}", [P, TPG])) for k in (2, 3)}

        ctx.enter_context(nc.Block())
        ready = Count(nc, ctx, "feed_constants")
        w_hi_ok = {name: Count(nc, ctx, name + "_hi_ok") for name in w}
        w_lo_ok = {name: Count(nc, ctx, name + "_lo_ok") for name in w}
        alone = ctx.enter_context(nc.semaphore("alone_feed"))
        sig = lambda name, per, eng, step=1, done=0: Signal(nc, ctx, name, per, eng, step, done)
        o_here, x1_here, x1_bo = sig("o_here", 1, sp, 16, 1), sig("x1_here", 1, sp, 16, 1), sig("x1_bo", 1, pool, 1, 1)
        ot_hi_ok, ot_lo_ok = sig("ot_hi_ok", 1, act, 1, 1), sig("ot_lo_ok", 1, pool, 1, 1)
        o_mm, o_read = sig("o_mm", TPG, pe), sig("o_read4", TPG, dve)
        ln = {k: dict(stat=sig(f"stat{k}", TPG, dve), mom=sig(f"mom{k}", TPG, dve), var=sig(f"var{k}", 1, dve),
                      rstd=sig(f"rstd{k}", 1, pool), done=sig(f"ln{k}", TPG, dve)) for k in (2, 3)}
        tr_mm, tr_read = sig("tr_mm4", TPG, pe), sig("tr_read", TPG, act)
        carried, diff_ok = sig("carried", 1, dve), sig("diff_ok", 1, dve)
        mix_ok = {g: sig("mixed_ok_" + g, 1, dve) for g in "kr"}
        mix_hi = {g: sig("mix_hi_" + g, 1, act) for g in "kr"}
        mix_lo = {"k": sig("mix_lo_k", 1, dve), "r": sig("mix_lo_r", 1, pool)}
        k_mm, k_relu, k_sq = sig("k_mm", 2, pe), sig("k_relu", 2, act), sig("k_sq", 2, dve)
        ka_hi, ka_lo = sig("ka_hi", 2, act), sig("ka_lo", 2, dve)
        r_mm, r_read = sig("r_mm", TPG, pe), sig("r_read", TPG, act)
        v_mm, v_read, v_sum = sig("v_mm", TPG, pe), sig("v_read", TPG, dve), sig("v_sum", TPG, dve)
        out_kept = sig("out_kept", 1, sp, 16)

        def stands_alone(engine):
            engine.sem_inc(alone, 1)

        def token0(b, j):
            return j * GT + b * S

        def load(n, b, j):
            ot_lo_ok.wait(sp, n - 1, 1)
            stands_alone(sp)
            o_here.by(sp.dma_start(o_in[:], o_dram.rearrange("(g p) n -> p g n", p=P)[:, :, bass.ds(token0(b, j), GT)]))
            o_read.wait(sp, n - 1, TPG)
            stands_alone(sp)
            x1_here.by(sp.dma_start(x1_in[:], x1_dram[bass.ds(token0(b, j), GT), :].rearrange("(t p) d -> p t d", p=P)))

        def take_in(n):
            o_here.wait(act, n, 1)
            o_mm.wait(act, n - 1, TPG)
            ot_hi_ok.by(act.activation(ot[0][:], o_in[:], ACT.Copy))
            ot_hi_ok.wait(pool, n, 1)
            o_mm.wait(pool, n - 1, TPG)
            ot_lo_ok.by(pool.tensor_tensor(ot[1][:], o_in[:], f32(ot[0][:]), ALU.subtract))

        def add_bias(n):
            x1_here.wait(pool, n, 1)
            x1_bo.by(pool.tensor_tensor(x1_in[:], x1_in[:], bo_row[:].unsqueeze(1).broadcast_to([P, TPG, D]), ALU.add))

        def row_product(bank, sta, weight, t):
            cols = slice(t * P, (t + 1) * P)
            for k in range(KT):
                m = three_pass(pe, bank[:], (sta[0][:, k, cols], sta[1][:, k, cols]),
                               (w[weight][0][:, k, :], w[weight][1][:, k, :]), first=(k == 0), last=(k == KT - 1))
            return m

        def moments(key, n, t, rows):
            st, mo, var, rs = norm[key]
            s = ln[key]
            s["stat"].by(dve.bn_stats(st[:, t, :], rows[:, t, :]))
            s["stat"].wait(dve, n, t + 1)
            stands_alone(dve)
            s["mom"].by(dve.bn_aggr(mo[:, t, :], st[:, t, :]))
            if t == TPG - 1:
                s["mom"].wait(dve, n, TPG)
                s["rstd"].wait(dve, n - 1, 1)
                s["var"].by(dve.tensor_scalar(var[:], mo[:, :, 1], EPS, None, ALU.add))
                s["var"].wait(pool, n, 1)
                s["done"].wait(pool, n - 1, TPG)
                s["rstd"].by(pool.tensor_tensor(rs[:], var[:], neg_half[:], ALU.pow))

        def normalise(key, n, rows):
            _, mo, _, rs = norm[key]
            ln[key]["rstd"].wait(dve, n, 1)
            for t in range(TPG):
                ln[key]["done"].by(dve.tensor_scalar(rows[:, t, :], rows[:, t, :], mo[:, t, 0:1], rs[:, t:t + 1],
                                                     ALU.subtract, ALU.mult))

        def o_product(n, t):
            ot_lo_ok.wait(pe, n, 1)
            o_read.wait(pe, n - 1, t + 1)
            o_mm.by(row_product(o_bank[t], ot, "cross_wo", t))

        def o_finish(n, b, t):
            o_mm.wait(dve, n, t + 1)
            x1_bo.wait(dve, n, 1)
            if t == 0 and not (isinstance(n, int) and n < B):
                tr_mm.wait(dve, n - B, TPG)
                v_sum.wait(dve, n - B, TPG)
            o_read.by(dve.tensor_tensor(x2[b][:, t, :], o_bank[t][:], x1_in[:, t, :], ALU.add))
            o_read.wait(dve, n, t + 1)
            moments(2, n, t, x2[b])

        def turn(n, b, t):
            ln[2]["done"].wait(pe, n, t + 1)
            tr_read.wait(pe, n - 1, t + 1)
            for k in range(KT):
                m = pe.transpose(tr_bank[t][:, k * P:(k + 1) * P], x2[b][:, t, k * P:(k + 1) * P], ident[:])
            tr_mm.by(m)

        def turned(n, b, t):
            tr_mm.wait(act, n, t + 1)
            carried.wait(act, n, 1)
            tr_read.by(act.activation(x2t[b][:, :, 1 + t * P:1 + (t + 1) * P],
                                      tr_bank[t][:].rearrange("p (k n) -> p k n", k=KT), ACT.Copy))

        def carry(n, b):
            mix_ok["r"].wait(dve, n - 1, 1)
            carried.by(dve.tensor_copy(x2t[b][:, :, 0:1], x2t[b][:, :, GT:GT + 1]))

        def blend(n, b, g):
            now, before = x2t[b][:, :, 1:1 + GT], x2t[b][:, :, 0:GT]
            if g == "k":
                tr_read.wait(dve, n, TPG)
                mix_ok["r"].wait(dve, n - 1, 1)
                diff_ok.by(dve.tensor_tensor(diff[:], now, before, ALU.subtract))
                diff_ok.wait(dve, n, 1)
            mix_lo[g].wait(dve, n - 1, 1)
            c0 = {"k": 5 * KT, "r": 4 * KT}[g]
            for k in range(KT):
                m = dve.scalar_tensor_tensor(mixed[g][:, k, :], diff[:, k, :], col_sb[:, c0 + k:c0 + k + 1],
                                             before[:, k, :], ALU.mult, ALU.add)
            mix_ok[g].by(m)
            mix_ok[g].wait(act, n, 1)
            last_mm = (k_mm, 2) if g == "k" else (r_mm, TPG)
            last_mm[0].wait(act, n - 1, last_mm[1])
            mix_hi[g].by(act.activation(mix[g][0][:], mixed[g][:], ACT.Copy))

        def blend_low(n, g):
            eng = dve if g == "k" else pool
            mix_hi[g].wait(eng, n, 1)
            mix_lo[g].by(eng.tensor_tensor(mix[g][1][:], mixed[g][:], f32(mix[g][0][:]), ALU.subtract))

        def k_product(n, h):
            mix_lo["k"].wait(pe, n, 1)
            k_sq.wait(pe, n - 1, h + 1)
            for i in range(2):
                cols = slice((2 * h + i) * P, (2 * h + i + 1) * P)
                for k in range(KT):
                    m = three_pass(pe, k_bank[h][:, i * GT:(i + 1) * GT],
                                   (w["ffn_wk"][0][:, k, cols], w["ffn_wk"][1][:, k, cols]),
                                   (mix["k"][0][:, k, :], mix["k"][1][:, k, :]), first=(k == 0), last=(k == KT - 1))
            k_mm.by(m)

        def k_finish(n, h):
            kt = slice(2 * h, 2 * h + 2)
            bank = k_bank[h][:].rearrange("p (k n) -> p k n", k=2)
            k_mm.wait(act, n, h + 1)
            k_sq.wait(act, n - 1, h + 1)
            k_relu.by(act.activation(relu[:, kt, :], bank, ACT.Relu))
            k_relu.wait(dve, n, h + 1)
            ka_lo.wait(dve, n - 1, h + 1)
            k_sq.by(dve.scalar_tensor_tensor(square[:, kt, :], bank, 0.0, relu[:, kt, :], ALU.max, ALU.mult))
            k_sq.wait(act, n, h + 1)
            v_mm.wait(act, n - 1, TPG)
            ka_hi.by(act.activation(ka[0][:, kt, :], square[:, kt, :], ACT.Copy))
            ka_hi.wait(dve, n, h + 1)
            ka_lo.by(dve.tensor_tensor(ka[1][:, kt, :], square[:, kt, :], f32(ka[0][:, kt, :]), ALU.subtract))

        def r_product(n, t):
            mix_lo["r"].wait(pe, n, 1)
            v_read.wait(pe, n - 1, t + 1)
            r_mm.by(row_product(rv_bank[t], mix["r"], "ffn_wr", t))

        def r_gate(n, t):
            r_mm.wait(act, n, t + 1)
            v_read.wait(act, n - 1, t + 1)
            r_read.by(act.activation(gate[:, t, :], rv_bank[t][:], ACT.Tanh, scale=0.5))

        def v_product(n, t):
            ka_lo.wait(pe, n, 2)
            r_read.wait(pe, n, t + 1)
            v_mm.by(row_product(rv_bank[t], ka, "ffn_wv", t))

        def v_finish(n, b, t):
            v_mm.wait(dve, n, t + 1)
            if t == 0:
                out_kept.wait(dve, n - 1, 1)
            v_read.by(dve.scalar_tensor_tensor(y3[:, t, :], gate[:, t, :], 1.0, rv_bank[t][:], ALU.add, ALU.mult))
            v_read.wait(dve, n, t + 1)
            v_sum.by(dve.scalar_tensor_tensor(y3[:, t, :], y3[:, t, :], 0.5, x2[b][:, t, :], ALU.mult, ALU.add))
            v_sum.wait(dve, n, t + 1)
            moments(3, n, t, y3)

        def store(n, b, j):
            ln[3]["done"].wait(sp, n, TPG)
            stands_alone(sp)
            out_kept.by(sp.dma_start(out[bass.ds(token0(b, j), GT), :].rearrange("(t p) d -> p t d", p=P), y3[:]))

        def group(n, b, j, ahead, ahead2):
            b1 = (b + 1) % B
            k_product(n, 0)
            if ahead:
                o_product(n + 1, 0)
                o_finish(n + 1, b1, 0)
            k_finish(n, 0)
            if ahead:
                o_product(n + 1, 1)
                o_finish(n + 1, b1, 1)
            if ahead2:
                load(n + 2, b, j + 1)
            k_product(n, 1)
            if ahead:
                normalise(2, n + 1, x2[b1])
                carry(n + 1, b1)
            k_finish(n, 1)
            r_product(n, 0)
            if ahead:
                for t in range(TPG):
                    turn(n + 1, b1, t)
                    turned(n + 1, b1, t)
            r_gate(n, 0)
            r_product(n, 1)
            if ahead2:
                take_in(n + 2)
                add_bias(n + 2)
            r_gate(n, 1)
            if ahead:
                blend(n + 1, b1, "k")
                blend_low(n + 1, "k")
            v_product(n, 0)
            v_finish(n, b, 0)
            v_product(n, 1)
            v_finish(n, b, 1)
            if ahead:
                blend(n + 1, b1, "r")
                blend_low(n + 1, "r")
            normalise(3, n, y3)
            store(n, b, j)

        o_kept.wait(sp, NG - 1, 1)
        for b in range(B):
            zero = ready.did(pool.memset(x2t[b][:], 0.0))
        zero = ready.did(pool.memset(neg_half[:], -0.5))
        ready.wait(dve, zero)
        ready.wait(pool, zero)

        def weight_high(name):
            raw_in[name].wait(act)
            w_hi_ok[name].did(act.activation(w[name][0][:], raw[name][:], ACT.Copy))

        def weight_low(name):
            raw_in[name].wait(dve)
            w_hi_ok[name].wait(dve)
            w_lo_ok[name].did(dve.tensor_tensor(w[name][1][:], raw[name][:], f32(w[name][0][:]), ALU.subtract))

        for name in FEED_WEIGHTS[1:]:
            weight_high(name)
        o_product(0, 0)
        weight_low("ffn_wk")
        o_finish(0, 0, 0)
        o_product(0, 1)
        weight_low("ffn_wr")
        o_finish(0, 0, 1)
        load(1, 1, 0)
        normalise(2, 0, x2[0])
        carry(0, 0)
        weight_low("ffn_wv")
        for t in range(TPG):
            turn(0, 0, t)
            turned(0, 0, t)
        take_in(1)
        for g in "kr":
            blend(0, 0, g)
            blend_low(0, g)
        add_bias(1)
        for name in FEED_WEIGHTS[1:]:
            w_lo_ok[name].wait(pe)
        with nc.Fori(0, NG // B - 1) as j:
            for b in range(B):
                group(B * j + b, b, j, True, True)
        last = NG // B - 1
        for b in range(B):
            group(B * last + b, b, last, b < B - 1, False)
        out_kept.wait(sp, NG - 1, 1)


def decoder_layer(nc, whole, io, out):
    from contextlib import ExitStack

    x1_dram = nc.dram_tensor("x1_scratch", (B * S, D), F32, kind="Internal").ap()
    o_dram = nc.dram_tensor("o_scratch", (D, B * S), F32, kind="Internal").ap()
    mem = Map(nc)
    pool, dve = nc.gpsimd, nc.vector
    ident = mem.place("ident", [P, P])
    ones = mem.place("ones", [P, P])
    col_sb = mem.place("cols", [P, len(COLS) * KT])
    keep = mem.at
    k_both, k_hi, k_lo = mem.joined_pair("k_blocks", [P, B, HG, GK], 2)
    v_both, v_hi, v_lo = mem.joined_pair("v_blocks", [P, B, CH, HG, P], 3)
    c_row = mem.place("c_row", [P, B, D])
    kept_kv = mem.at
    wq_hi, wq_lo = mem.pair("cross_wq", [P, KT, D])
    x_in = mem.place("x_cols_in", [P, KT, GT])
    xt_hi, xt_lo = mem.pair("xt", [P, KT, GT])
    early, behind_early = (wq_hi, wq_lo, x_in, xt_hi, xt_lo), mem.at
    mem.at = kept_kv
    fold_w = {n: mem.place(n, [P, KT, D]) for n in ("self_wv", "self_wk")}
    x_sum = mem.place("x_sum", [P, B, D])
    fold_w |= {n: mem.place(n, [P, KT, D]) for n in ("self_wo", "self_wq")}
    kept_fold = mem.at
    kv = (k_hi, k_lo, v_hi, v_lo, x_sum, k_both, v_both)

    with ExitStack() as ctx:
        made = Count(nc, ctx, "consts")
        ctx.enter_context(nc.Block())
        zero = made.did(pool.memset(ident[:], 0.0))
        made.wait(pool, zero)
        made.did(pool.affine_select(out=ident[:], in_=ident[:], compare_op=ALU.not_equal, fill=1.0, base=0,
                                    pattern=[[-1, P]], channel_multiplier=1))
        made.did(pool.memset(ones[:], 1.0))
        o_kept = Signal(nc, whole, "o_kept", 1, nc.sync, 16)
    io = {**io, "ident": ident, "ones": ones}

    with ExitStack() as ctx:
        banks = [ctx.enter_context(nc.psum_tensor(f"bank{i}", [P, D], F32)) for i in range(8)]
        gram = [banks[0:4], banks[4:8]]
        top = mem.end
        m_base = (top - 2 * B * KT * D * 4) // 32 * 32
        placements = context_and_gram(nc, io, mem, kv, col_sb, gram, fold_w, m_base)
        mem.at = m_base
        m_hi, m_lo = mem.pair("m", [P, B, KT, D])
        mem.at = m_base - KT * D * 4
        w_q_raw = mem.place("w_q_raw", [P, KT, D])
        mem.at, mem.end = kept_fold, m_base - KT * D * 4
        fold(nc, io, mem, kv, col_sb, gram, banks, fold_w, (m_hi, m_lo), c_row, w_q_raw, placements,
             early)
    feed_raw_in = {name: Count(nc, whole, name + "_in", 16) for name in FEED_WEIGHTS}
    with ExitStack() as ctx:
        scores = ctx.enter_context(nc.psum_tensor("scores", [P, 2, D], F32))
        turned = [ctx.enter_context(nc.psum_tensor(f"turned{i}", [P, 2 * D], F32)) for i in range(2)]
        value = ctx.enter_context(nc.psum_tensor("value", [P, D], F32))
        nxt = ctx.enter_context(nc.psum_tensor("next", [P, D], F32))
        mem.at, mem.end = kept_kv, top
        wo = mem.pair("cross_wo", [P, KT, D])
        o_in = mem.place("o_in", [P, HG, GT])
        ot = mem.pair("o_t", [P, HG, GT])
        x1_in = mem.place("x1_in", [P, TPG, D])
        behind_first = mem.at
        mem.at = kept_kv - B * D * 4
        bo_row = mem.place("cross_bo_row", [P, D])
        feed_first = (*wo, o_in, *ot, x1_in, bo_row)
        mem.at = m_base
        feed_raw = {name: mem.place(name + "_raw", [P, KT, D]) for name in FEED_WEIGHTS}
        mem.at, mem.end = behind_early, m_base
        attend(nc, io, mem, kv, col_sb, {"scores": scores, "turned": turned, "value": value, "next": nxt},
               (m_hi, m_lo), c_row, early, (x1_dram, o_dram), feed_raw, feed_raw_in,
               feed_first, o_kept)
    with ExitStack() as ctx:
        banks = [ctx.enter_context(nc.psum_tensor(f"feed_bank{i}", [P, D], F32)) for i in range(8)]
        mem.at, mem.end = keep, m_base - HG * GT * 4
        feed(nc, io, mem, col_sb, banks, (x1_dram, o_dram), feed_raw, feed_raw_in, feed_first,
             (kept_kv - B * D * 4, behind_first), o_kept, out)


def kernel(**inputs):
    from contextlib import ExitStack
    import concourse.bacc as bacc
    from concourse.bass_utils import run_bass_kernel_spmd

    a = {k: np.asarray(v) for k, v in inputs.items()}
    flat = np.ascontiguousarray
    heads = D // SELF_DH
    by_head = lambda w: w.reshape((3, SELF_DH, heads) + w.shape[1:]).swapaxes(1, 2).reshape((3, D) + w.shape[1:])
    w_q, w_k, w_v = by_head(a["L0_attn_w_qkv"])
    b_q, b_k, b_v = by_head(a["L0_attn_b_qkv"])
    cols = {"self_bq": b_q, "self_bv": b_v, "cross_bq": a["L0_xattn_b_q"], "cross_bk": a["L0_xattn_b_k"],
            "mu_r": a["L0_ffn_mu_r"], "mu_k": a["L0_ffn_mu_k"]}
    rows = {"self_bk": b_k, "self_bv_row": b_v, "self_bo": a["L0_attn_b_o"], "cross_bv": a["L0_xattn_b_v"],
            "cross_bo": a["L0_xattn_b_o"]}
    arrays = {
        "x_rows": flat(a["x"].reshape(B * S, D)),
        "x_cols": flat(a["x"].reshape(B * S, D).T),
        "ctx_cols": flat(a["ctx_1024"].reshape(B * CTX, D).T),
        "mask": flat(a["mask_Bx1xSxS2_ik1"].reshape(B * S, CTX)),
        "cols": flat(np.concatenate([cols[c].reshape(KT, P).T for c in COLS], axis=1)),
        "rows": flat(np.stack([rows[r] for r in ROWS])),
        "self_wq": flat(w_q), "self_wk": flat(w_k.T), "self_wv": flat(w_v.T), "self_wo": flat(a["L0_attn_w_o"].T),
        "cross_wq": flat(a["L0_xattn_W_q"].T), "cross_wk": flat(a["L0_xattn_W_k"].T),
        "cross_wv": flat(a["L0_xattn_W_v"].T), "cross_wo": flat(a["L0_xattn_W_o"].T),
        "ffn_wr": flat(a["L0_ffn_W_r"].T), "ffn_wk": flat(a["L0_ffn_W_k"].T), "ffn_wv": flat(a["L0_ffn_W_v"].T),
    }
    nc = bacc.Bacc("TRN2", target_bir_lowering=False, num_devices=1)
    io = {n: nc.dram_tensor(n, v.shape, mybir.dt.from_np(v.dtype), kind="ExternalInput").ap() for n, v in arrays.items()}
    out = nc.dram_tensor("out", (B * S, D), F32, kind="ExternalOutput").ap()
    with ExitStack() as whole:
        decoder_layer(nc, whole, io, out)
    r = run_bass_kernel_spmd(nc, [arrays], core_ids=[0])
    return r.results[0]["out"].reshape(B, S, D)
```
